# Optimizing a Trainium2 kernel written in Bass

```python
import numpy as np
import jax
import jax.numpy as jnp

def _softmax(x, axis=-1):
    return jax.nn.softmax(x, axis=axis)

def _gelu(x):
    return jax.nn.gelu(x, approximate=True)

def _silu(x):
    return jax.nn.silu(x)

def _sigmoid(x):
    return jax.nn.sigmoid(x)

def _layernorm(x, axis=-1, eps=1e-05):
    m = jnp.mean(x, axis=axis, keepdims=True)
    v = jnp.var(x, axis=axis, keepdims=True)
    return (x - m) / jnp.sqrt(v + eps)

def _scatter_add(tgt, idx, src, axis=0):
    return tgt.at[idx].add(src)

def _segment_sum(src, seg, n):
    return jax.ops.segment_sum(src, seg, n)
kernel_name = 'mk_adj_preln_d1_adj_r2_9f0a53'

def setup_inputs(seed: int=0):
    np.random.seed(seed)
    _w = jnp.asarray

    def _rec_inputs():
        import jax
        import jax.numpy as jnp
        _gk = jax.random.key(seed)
        x = -0.0002928 + 1 * jax.random.normal(jax.random.fold_in(_gk, 1), (64, 128, 128), jnp.float32)
        _w = (1.0 + jnp.arange(128, dtype=jnp.float32)) ** (-0.5)
        _w = _w / _w.mean()
        _pij = jnp.clip(0.03125 * _w[:, None] * _w[None, :], 0.0, 1.0)
        _a = jax.random.uniform(jax.random.fold_in(_gk, 2), (64, 128, 128)) < _pij
        adj = _a.astype(jnp.int32)
        return (x, adj)
    x, adj = _rec_inputs()

    def _L0_gnn_setup():
        import jax, jax.numpy as jnp
        import numpy as np
        OUT = 128
        NUM_LAYERS = 3

        def _gru_cell(inp, h, w_ih, w_hh, b_ih, b_hh):
            gi = inp @ w_ih.T + b_ih
            gh = h @ w_hh.T + b_hh
            i_r, i_z, i_n = jnp.split(gi, 3, axis=-1)
            h_r, h_z, h_n = jnp.split(gh, 3, axis=-1)
            r = jax.nn.sigmoid(i_r + h_r)
            z = jax.nn.sigmoid(i_z + h_z)
            n = jnp.tanh(i_n + r * h_n)
            return (1.0 - z) * n + z * h
        key = jax.random.key(seed)
        ks = jax.random.split(key, 8)
        B, N, D = (32, 256, 128)
        x = jax.random.normal(ks[0], (B, N, D), dtype=jnp.float32)
        adj = jax.random.randint(ks[1], (B, N, N), 0, 2, dtype=jnp.int32)
        s = 1.0 / np.sqrt(OUT)
        weight = jax.random.uniform(ks[2], (NUM_LAYERS, OUT, OUT), jnp.float32, -s, s)
        w_ih = jax.random.uniform(ks[3], (3 * OUT, OUT), jnp.float32, -s, s)
        w_hh = jax.random.uniform(ks[4], (3 * OUT, OUT), jnp.float32, -s, s)
        b_ih = jax.random.uniform(ks[5], (3 * OUT,), jnp.float32, -s, s)
        b_hh = jax.random.uniform(ks[6], (3 * OUT,), jnp.float32, -s, s)
        return {'x': x, 'adj': adj, 'weight': weight, 'w_ih': w_ih, 'w_hh': w_hh, 'b_ih': b_ih, 'b_hh': b_hh}
    _L0_gnn_all = _L0_gnn_setup()
    _L0_gnn_in = {k: v for k, v in _L0_gnn_all.items() if k in ('weight', 'w_ih', 'w_hh', 'b_ih', 'b_hh')}
    del _L0_gnn_all
    return {'x': x, 'adj': adj, 'L0_gnn_weight': _L0_gnn_in['weight'], 'L0_gnn_w_ih': _L0_gnn_in['w_ih'], 'L0_gnn_w_hh': _L0_gnn_in['w_hh'], 'L0_gnn_b_ih': _L0_gnn_in['b_ih'], 'L0_gnn_b_hh': _L0_gnn_in['b_hh']}

def reference(x, adj, L0_gnn_weight, L0_gnn_w_ih, L0_gnn_w_hh, L0_gnn_b_ih, L0_gnn_b_hh):
    import jax
    import jax.numpy as jnp

    def _L0_gnn_ref(x, adj, weight, w_ih, w_hh, b_ih, b_hh):
        import jax, jax.numpy as jnp
        import numpy as np
        OUT = 128
        NUM_LAYERS = 3

        def _gru_cell(inp, h, w_ih, w_hh, b_ih, b_hh):
            gi = inp @ w_ih.T + b_ih
            gh = h @ w_hh.T + b_hh
            i_r, i_z, i_n = jnp.split(gi, 3, axis=-1)
            h_r, h_z, h_n = jnp.split(gh, 3, axis=-1)
            r = jax.nn.sigmoid(i_r + h_r)
            z = jax.nn.sigmoid(i_z + h_z)
            n = jnp.tanh(i_n + r * h_n)
            return (1.0 - z) * n + z * h
        A = (adj != 0).astype(x.dtype)
        h = x
        L = weight.shape[0]
        for i in range(L):
            m = jnp.einsum('bnd,de->bne', h, weight[i])
            aggr = jnp.einsum('bst,bsd->btd', A, m)
            h = _gru_cell(aggr, h, w_ih, w_hh, b_ih, b_hh)
        return h
    h = jnp.maximum(_layernorm(x, axis=-1), 0.0)
    x = x + _L0_gnn_ref(h, adj, L0_gnn_weight, L0_gnn_w_ih, L0_gnn_w_hh, L0_gnn_b_ih, L0_gnn_b_hh)
    return x

_drawn_inputs = setup_inputs


def setup_inputs(seed=0):
    import zlib

    import numpy as np

    out = dict(_drawn_inputs(seed))
    spreads = {}
    factors = {}
    for name, (base, spread) in spreads.items():
        noise = np.random.default_rng([zlib.crc32(name.encode()), seed]).standard_normal(out[name].shape)
        drawn = base * np.exp(spread * noise) if base else spread * noise
        out[name] = jnp.asarray(drawn.astype(out[name].dtype))
    for name, factor in factors.items():
        out[name] = (out[name] * factor).astype(out[name].dtype)
    return out
```

```python
from contextlib import ExitStack

import concourse.bass as bass
from concourse import mybir

F32 = mybir.dt.float32
F16 = mybir.dt.float16
I32 = mybir.dt.int32
ALU = mybir.AluOpType
ACT = mybir.ActivationFunctionType
AX_X = mybir.AxisListType.X

P = 128
GPG = 4
N = GPG * P
LAYERS = 3
R, Z, NN = range(3)
GATES = 3
WHH = LAYERS
SLOTS_W = LAYERS + 1
EPS = 1e-5
H_SCALE = 2.0 ** 11
U_SCALE = 2.0 ** -6
W_TOP = 2.0 ** 13
EXPONENT_BITS = 0x7F800000

POS = 2 * LAYERS


class Item:

    def __init__(self, n, k, layer, ab):
        self.n, self.layer, self.ab = n, layer, ab
        self.pair = k - layer
        self.group = 2 * self.pair + ab


class Step:

    def __init__(self, pos, item, back, early, early_before):
        self.pos, self.item, self.back = pos, item, back
        self.early, self.early_before = early, early_before


def slot_items(t, pairs):
    return [(l, ab) for l in (3, 2, 1) for ab in (0, 1) if 0 <= t - l < pairs]


def slot_steps(t, k, pairs):
    first = sum(len(slot_items(s, pairs)) for s in range(t))
    base = first if isinstance(k, int) else k * POS - (t * POS - first)
    order = [(s, l, ab) for s in range(max(t - 3, 0), t + 1) for l, ab in slot_items(s, pairs)]
    here = len(order) - len(slot_items(t, pairs))
    n_of = {item: i - here for i, item in enumerate(order)}

    def item(i):
        if not 0 <= i < len(order):
            return None
        s, l, ab = order[i]
        return Item(base + (i - here), k + (s - t), l, ab)

    def early(i):
        if not 0 <= i < len(order):
            return False
        s, l, ab = order[i]
        return l > 1 and n_of.get((s - 1, l - 1, ab), -99) == i - here - 2

    steps = []
    for pos in range(POS):
        l, ab = 3 - pos // 2, pos % 2
        i = order.index((t, l, ab)) if (t, l, ab) in order else None
        if i is None:
            steps.append(Step(pos, None, [None] * 4, False, False))
        else:
            steps.append(Step(pos, item(i), [item(i - j) for j in range(4)], early(i), early(i - 1)))
    return steps


def drain_steps(t, pairs):
    order = [(t, l, ab) for l, ab in slot_items(t, pairs)]
    total = sum(len(slot_items(s, pairs)) for s in range(t + 1))
    last = [Item(total - len(order) + i, t, l, ab) for i, (_, l, ab) in enumerate(order)]
    for j in range(1, 4):
        back = [None] * 4
        for b in range(j, 4):
            if 0 <= len(last) - 1 + j - b < len(last):
                back[b] = last[len(last) - 1 + j - b]
        yield Step(None, None, back, True, True)


def build(nc, x, adj, weight, w_ih, w_hh, b_ih, b_hh, out):
    graphs = x.shape[0]
    groups = graphs // GPG
    pairs = groups // 2
    steady = range(LAYERS, pairs)
    last_slot = pairs + LAYERS - 1

    with ExitStack() as ctx:
        def sb(name, shape, dt):
            return ctx.enter_context(nc.sbuf_tensor(name, shape, dt))

        def psum(name):
            return ctx.enter_context(nc.psum_tensor(name, [P, N], F32))

        def sem(name):
            return ctx.enter_context(nc.semaphore(name))

        ps_r, ps_z, ps_hn = psum("ps_r"), psum("ps_z"), psum("ps_hn")
        ps_in = [psum("ps_in0"), psum("ps_in1")]
        ps_u, ps_turn, ps_turn0 = psum("ps_u"), psum("ps_turn"), psum("ps_turn0")

        def halves(bank):
            return bank[:, :].bitcast(F16).rearrange("p (c n) -> p c n", c=2)

        x_all = sb("x_all", [P, graphs * P], F32)
        adj_int = sb("adj_int", [P, graphs * P], I32)
        adj_one = sb("adj_one", [P, graphs * P], F16)
        ident = sb("ident", [P, P], F32)
        ident16 = sb("ident16", [P, P], F16)
        ident_out = sb("ident_out", [P, P], F16)
        wih_rows = sb("wih_rows", [P, GATES, P], F32)
        wl_rows = sb("wl_rows", [P, LAYERS, P], F32)
        wih_t = sb("wih_t", [P, GATES, P], F32)
        wl_t = sb("wl_t", [P, LAYERS, P], F32)
        w_rows = sb("w_rows", [P, GATES, SLOTS_W, P], F32)
        w_hi = sb("w_hi", [P, GATES, SLOTS_W, P], F16)
        w_lo = sb("w_lo", [P, GATES, SLOTS_W, P], F16)
        bias_rows = sb("bias_rows", [2 * GATES, P], F32)
        biases = sb("biases", [P, 2 * GATES], F32)
        bias_ih, bias_hh = biases[:, 0:GATES], biases[:, GATES:2 * GATES]
        w_top = sb("w_top", [P, GATES], F32)
        w_scale = sb("w_scale", [P, GATES], F32)
        back_scale = sb("back_scale", [P, GATES], F32)
        gate_bias = sb("gate_bias", [P, GATES], F32)
        neg_scale = sb("neg_scale", [P, 1], F32)
        bhn_scaled = sb("bhn_scaled", [P, 1], F32)
        half_neg = sb("half_neg", [P, GPG], F32)
        stats = sb("stats", [P, 2, GPG, 6], F32)
        moments = sb("moments", [P, 2, GPG, 2], F32)
        var_eps = sb("var_eps", [P, 2, GPG], F32)
        inv_std = sb("inv_std", [P, 2, GPG], F32)
        normed = sb("normed", [P, 2, N], F32)
        state = sb("state", [P, LAYERS + 1, 2, N], F32)
        state16 = sb("state16", [P, LAYERS + 1, 2, 2, N], F16)
        nodes16 = sb("nodes16", [P, LAYERS, 2, 2, N], F16)
        u16 = sb("u16", [P, 2, N], F16)
        r_sb = sb("r_sb", [P, N], F32)
        z_sb = sb("z_sb", [P, 2, N], F32)
        rn_sb = sb("rn_sb", [P, N], F32)
        diff = sb("diff", [P, 2, N], F32)
        step_sb = sb("step_sb", [P, N], F32)

        s_w, s_x, s_adj, s_store = sem("s_w"), sem("s_x"), sem("s_adj"), sem("s_store")
        s_zero, s_ident, s_ident16, s_scale, s_bias = (
            sem("s_zero"), sem("s_ident"), sem("s_ident16"), sem("s_scale"), sem("s_bias"))
        s_wt, s_wt_sb, s_prod = sem("s_wt"), sem("s_wt_sb"), sem("s_prod")
        s_rows, s_const, s_wturn, s_whi, s_wlo = (
            sem("s_rows"), sem("s_const"), sem("s_wturn"), sem("s_whi"), sem("s_wlo"))
        s_bn, s_mom, s_var, s_inv, s_normed, s_one = (
            sem("s_bn"), sem("s_mom"), sem("s_var"), sem("s_inv"), sem("s_normed"), sem("s_one"))
        s_hi0, s_nodes0, s_turn0, s_state16_0, s_state0 = (
            sem("s_hi0"), sem("s_nodes0"), sem("s_turn0"), sem("s_state16_0"), sem("s_state0"))
        s_agg, s_uhi, s_ulo = sem("s_agg"), sem("s_uhi"), sem("s_ulo")
        s_pr, s_pn, s_pz = sem("s_pr"), sem("s_pn"), sem("s_pz")
        s_r, s_z, s_rn, s_nsum, s_tanh = sem("s_r"), sem("s_z"), sem("s_rn"), sem("s_nsum"), sem("s_tanh")
        s_diff, s_step, s_state, s_hi, s_lo = (
            sem("s_diff"), sem("s_step"), sem("s_state"), sem("s_hi"), sem("s_lo"))
        s_turn = sem("s_turn")
        s_taken = [None] + [sem(f"s_taken{l}") for l in range(1, LAYERS + 1)]

        block = ctx.enter_context(nc.Block())

        def wait_before(eng, s, value):
            if isinstance(value, int) and value <= 0:
                return
            eng.wait_ge(s, value)

        def slots(eng, slot):
            for t in range(steady.start):
                slot(t, t)
            with eng.Fori(steady.start, steady.stop) as k:
                slot(steady.start, k)
            for t in range(steady.stop, last_slot + 1):
                slot(t, t)

        def group_columns(group):
            return bass.ds(group * N, N)

        @block.sync
        def _(sp):
            x_src = x.rearrange("g n d -> n g d")
            adj_src = adj.rearrange("g s t -> s g t")
            out_dst = out.rearrange("g n d -> n g d")
            pair_graphs = 2 * GPG

            def load(k):
                first = k * pair_graphs if isinstance(k, int) else sp.snap(k * pair_graphs)
                cols = bass.ds(first * P, 2 * N)
                src = bass.ds(first, pair_graphs)
                wait_before(sp, s_x, k * 16)
                wait_before(sp, s_adj, k * 16)
                sp.dma_start(x_all[:, cols].rearrange("p (g d) -> p g d", d=P), x_src[:, src, :]).then_inc(s_x, 16)
                if isinstance(k, int):
                    sp.dma_start(wih_rows[:, :, :], w_ih.rearrange("(g e) f -> e g f", e=P)).then_inc(s_w, 16)
                    sp.dma_start(wl_rows[:, :, :], weight.rearrange("l d f -> d l f")).then_inc(s_w, 16)
                    sp.dma_start(w_rows[:, :, WHH, :], w_hh.rearrange("(g e) f -> e g f", e=P)).then_inc(s_w, 16)
                    sp.dma_start(bias_rows[0:GATES, :], b_ih.rearrange("(g e) -> g e", e=P)).then_inc(s_w, 16)
                    sp.dma_start(bias_rows[GATES:2 * GATES, :], b_hh.rearrange("(g e) -> g e", e=P)).then_inc(s_w, 16)
                sp.dma_start(adj_int[:, cols].rearrange("p (g d) -> p g d", d=P), adj_src[:, src, :]).then_inc(s_adj, 16)

            load(0)
            with sp.Fori(1, pairs) as k:
                load(k)
            with sp.Fori(0, groups) as g:
                sp.wait_ge(s_taken[LAYERS], g + 1)
                sp.dma_start(out_dst[:, bass.ds(g * GPG, GPG), :],
                             x_all[:, group_columns(g)].rearrange("p (g d) -> p g d", d=P)).then_inc(s_store, 16)
            sp.wait_ge(s_store, groups * 16)

        @block.tensor
        def _(pe):
            def product(bank, gate, slot, hi, lo, first, last):
                wh, wl = w_hi[:, gate, slot, :], w_lo[:, gate, slot, :]
                pe.matmul(bank[:, :], wh, hi, start=first, stop=False)
                pe.matmul(bank[:, :], wh, lo, start=False, stop=False)
                return pe.matmul(bank[:, :], wl, hi, start=False, stop=last)

            def setup():
                pe.wait_ge(s_w, 5 * 16)
                pe.wait_ge(s_ident, 1)
                for g in range(GATES):
                    pe.transpose(ps_r[:, g * P:(g + 1) * P], wih_rows[:, g, :], ident[:, :])
                for l in range(LAYERS):
                    m = pe.transpose(ps_z[:, l * P:(l + 1) * P], wl_rows[:, l, :], ident[:, :])
                m = pe.transpose(ps_u[:, 0:2 * GATES], bias_rows[:, :], ident[0:2 * GATES, 0:2 * GATES])
                m.then_inc(s_wt, 1)
                pe.wait_ge(s_wt_sb, 2)
                for g, bank in enumerate((ps_hn, ps_in[0], ps_in[1])):
                    pe.matmul(bank[:, 0:LAYERS * P], wih_t[:, g, :], wl_t[:, :, :].rearrange("p l d -> p (l d)"),
                              start=True, stop=True).then_inc(s_prod, 1)
                for g, bank in enumerate((ps_r, ps_z, ps_u)):
                    pe.wait_ge(s_rows, GATES + 1 + g)
                    for s in range(SLOTS_W):
                        m = pe.transpose(bank[:, s * P:(s + 1) * P], w_rows[:, g, s, :], ident[:, :])
                    m.then_inc(s_wturn, 1)
                pe.wait_ge(s_wlo, GATES)
                pe.wait_ge(s_ident16, 3)

            def aggregate(it):
                l, ab = it.layer, it.ab
                if l == 1:
                    pe.wait_ge(s_nodes0, it.group + 1)
                    pe.wait_ge(s_one, it.group + 1)
                else:
                    pe.wait_ge(s_taken[l - 1], it.group + 1)
                wait_before(pe, s_ulo, it.n)
                for b in range(GPG):
                    cols = slice(b * P, (b + 1) * P)
                    a = adj_one[:, bass.ds(it.group * N + b * P, P)]
                    pe.matmul(ps_u[:, cols], nodes16[:, l - 1, ab, 0, cols], a, start=True, stop=False)
                    m = pe.matmul(ps_u[:, cols], nodes16[:, l - 1, ab, 1, cols], a, start=False, stop=True)
                m.then_inc(s_agg, 1)

            def hidden_part(it):
                hi, lo = (state16[:, it.layer - 1, it.ab, c, :] for c in (0, 1))
                if it.layer == 1:
                    pe.wait_ge(s_state16_0, it.group + 1)
                wait_before(pe, s_r, it.n)
                product(ps_r, R, WHH, hi, lo, True, False)
                wait_before(pe, s_rn, it.n)
                product(ps_hn, NN, WHH, hi, lo, True, True)
                wait_before(pe, s_z, it.n)
                product(ps_z, Z, WHH, hi, lo, True, False)

            def input_part(it):
                hi, lo, s = u16[:, 0, :], u16[:, 1, :], it.layer - 1
                pe.wait_ge(s_ulo, it.n + 1)
                product(ps_r, R, s, hi, lo, False, True).then_inc(s_pr, 1)
                wait_before(pe, s_diff, it.n - 1)
                product(ps_in[parity(it)], NN, s, hi, lo, True, True).then_inc(s_pn, 1)
                product(ps_z, Z, s, hi, lo, False, True).then_inc(s_pz, 1)

            def turn(it, before):
                l, ab = it.layer, it.ab
                pe.wait_ge(s_lo, it.n + 1)
                if before is not None:
                    pe.wait_ge(s_taken[before.layer], before.group + 1)
                for b in range(GPG):
                    cols = slice(b * P, (b + 1) * P)
                    for c in (0, 1):
                        part = state16[:, l, ab, c, cols]
                        if l < LAYERS:
                            m = pe.transpose(halves(ps_turn)[:, c, cols], part, ident16[:, :])
                        else:
                            m = pe.matmul(ps_turn[:, cols], part, ident_out[:, :], start=(c == 0), stop=(c == 1))
                m.then_inc(s_turn, 1)

            def turn_normed(group, ab):
                pe.wait_ge(s_nodes0, group + 1)
                wait_before(pe, s_state16_0, group)
                for b in range(GPG):
                    cols = slice(b * P, (b + 1) * P)
                    for c in (0, 1):
                        m = pe.transpose(halves(ps_turn0)[:, c, cols], nodes16[:, 0, ab, c, cols], ident16[:, :])
                m.then_inc(s_turn0, 1)

            def slot(t, k):
                for st in slot_steps(t, k, pairs):
                    if st.item is not None:
                        if st.early and st.back[2] is not None:
                            turn(st.back[2], st.back[3])
                        aggregate(st.item)
                        hidden_part(st.item)
                        input_part(st.item)
                        if not st.early and st.back[2] is not None:
                            turn(st.back[2], st.back[3])
                    if st.pos in (1, 2) and 0 <= t - 1 < pairs:
                        turn_normed(2 * (k - 1) + st.pos - 1, st.pos - 1)

            setup()
            slots(pe, slot)
            for st in drain_steps(last_slot, pairs):
                if st.back[2] is not None:
                    turn(st.back[2], st.back[3])

        @block.scalar
        def _(act):
            def setup():
                act.wait_ge(s_wt, 1)
                act.activation(wih_t[:, :, :].rearrange("p g e -> p (g e)"), ps_r[:, 0:GATES * P],
                               ACT.Copy).then_inc(s_wt_sb, 1)
                for g, bank in enumerate((ps_hn, ps_in[0], ps_in[1])):
                    act.wait_ge(s_prod, g + 1)
                    act.activation(w_rows[:, g, 0:LAYERS, :].rearrange("p l d -> p (l d)"), bank[:, 0:LAYERS * P],
                                   ACT.Copy, scale=1.0 / U_SCALE).then_inc(s_rows, 1)
                for g, bank in enumerate((ps_r, ps_z, ps_u)):
                    act.wait_ge(s_wturn, g + 1)
                    act.activation(w_hi[:, g, :, :].rearrange("p s e -> p (s e)"), bank[:, :],
                                   ACT.Copy).then_inc(s_whi, 1)
                act.wait_ge(s_const, 3)

            def gate_z(it):
                act.wait_ge(s_pz, it.n + 1)
                wait_before(act, s_step, it.n - 1)
                act.activation(z_sb[:, parity(it), :], ps_z[:, :], ACT.Sigmoid,
                               bias=gate_bias[:, Z:Z + 1], scale=neg_scale[:, :]).then_inc(s_z, 1)

            def gate_r(it):
                act.wait_ge(s_pr, it.n + 1)
                wait_before(act, s_rn, it.n)
                act.activation(r_sb[:, :], ps_r[:, :], ACT.Sigmoid,
                               bias=gate_bias[:, R:R + 1], scale=back_scale[:, R:R + 1]).then_inc(s_r, 1)

            def gate_n(it):
                act.wait_ge(s_nsum, it.n + 1)
                bank = ps_in[parity(it)]
                act.activation(bank[:, :], bank[:, :], ACT.Tanh,
                               bias=biases[:, NN:NN + 1], scale=back_scale[:, NN:NN + 1]).then_inc(s_tanh, 1)

            def u_hi(it):
                act.wait_ge(s_agg, it.n + 1)
                act.activation(u16[:, 0, :], ps_u[:, :], ACT.Copy, scale=U_SCALE).then_inc(s_uhi, 1)

            def state_hi(it):
                act.wait_ge(s_state, it.n + 1)
                act.activation(state16[:, it.layer, it.ab, 0, :], state[:, it.layer, it.ab, :],
                               ACT.Copy).then_inc(s_hi, 1)

            def take_turned(it):
                act.wait_ge(s_turn, it.n + 1)
                act.activation(nodes16[:, it.layer, it.ab, :, :].rearrange("p c n -> p (c n)"),
                               ps_turn[:, :].bitcast(F16), ACT.Copy).then_inc(s_taken[it.layer], 1)

            def take_normed(group, ab):
                act.wait_ge(s_turn0, group + 1)
                act.activation(state16[:, 0, ab, :, :].rearrange("p c n -> p (c n)"),
                               ps_turn0[:, :].bitcast(F16), ACT.Copy).then_inc(s_state16_0, 1)

            def slot(t, k):
                for st in slot_steps(t, k, pairs):
                    if st.item is not None:
                        _, b1, b2, b3 = st.back
                        if b1 is not None:
                            gate_z(b1)
                        if st.early:
                            if b3 is not None and not st.early_before and b3.layer < LAYERS:
                                take_turned(b3)
                            state_hi(b2)
                            if b2.layer < LAYERS:
                                take_turned(b2)
                        u_hi(st.item)
                        if b1 is not None:
                            gate_n(b1)
                        if not st.early:
                            if b2 is not None:
                                state_hi(b2)
                            if b3 is not None and not st.early_before and b3.layer < LAYERS:
                                take_turned(b3)
                        gate_r(st.item)
                    if st.pos in (2, 3) and 0 <= t - 1 < pairs:
                        take_normed(2 * (k - 1) + st.pos - 2, st.pos - 2)

            setup()
            slots(act, slot)
            for st in drain_steps(last_slot, pairs):
                _, b1, b2, b3 = st.back
                if b1 is not None:
                    gate_z(b1)
                    gate_n(b1)
                if b2 is not None:
                    state_hi(b2)

        @block.vector
        def _(dve):
            def setup():
                dve.memset(half_neg[:, :], -0.5).then_inc(s_ident16, 1)
                dve.wait_ge(s_ident, 1)
                dve.tensor_copy(ident16[:, :], ident[:, :]).then_inc(s_ident16, 1)
                dve.tensor_scalar(ident_out[:, :], ident[:, :], 1.0 / H_SCALE, None, ALU.mult).then_inc(s_ident16, 1)

            def setup_weights():
                dve.wait_ge(s_wt, 1)
                dve.tensor_copy(wl_t[:, :, :].rearrange("p l d -> p (l d)"), ps_z[:, 0:LAYERS * P]).then_inc(s_wt_sb, 1)
                dve.tensor_copy(biases[:, :], ps_u[:, 0:2 * GATES]).then_inc(s_bias, 1)
                for g in range(GATES):
                    dve.wait_ge(s_rows, g + 1)
                    dve.tensor_reduce(w_top[:, g:g + 1], w_rows[:, g, :, :].rearrange("p s d -> p (s d)"),
                                      AX_X, ALU.max, apply_absolute_value=True).then_inc(s_scale, 1)
                dve.wait_ge(s_scale, GATES)
                dve.tensor_scalar(w_top[:, :], w_top[:, :], 2.0 ** -60, 2.0 ** 60, ALU.max, ALU.min).then_inc(s_scale, 1)
                dve.wait_ge(s_scale, GATES + 1)
                top_bits = w_top[:, :].bitcast(I32)
                dve.tensor_scalar(top_bits, top_bits, EXPONENT_BITS, None, ALU.bitwise_and).then_inc(s_scale, 1)
                dve.wait_ge(s_scale, GATES + 2)
                dve.reciprocal(w_scale[:, :], w_top[:, :]).then_inc(s_scale, 1)
                dve.tensor_scalar(back_scale[:, :], w_top[:, :], 1.0 / (W_TOP * H_SCALE), None, ALU.mult).then_inc(s_scale, 1)
                dve.wait_ge(s_scale, GATES + 4)
                for g in range(GATES):
                    rows = w_rows[:, g, :, :].rearrange("p s d -> p (s d)")
                    dve.tensor_scalar(rows, rows, w_scale[:, g:g + 1], W_TOP, ALU.mult, ALU.mult).then_inc(s_rows, 1)
                for g, bank in enumerate((ps_r, ps_z, ps_u)):
                    dve.wait_ge(s_whi, g + 1)
                    dve.tensor_tensor(w_lo[:, g, :, :].rearrange("p s e -> p (s e)"), bank[:, :],
                                      w_hi[:, g, :, :].rearrange("p s e -> p (s e)"), ALU.subtract).then_inc(s_wlo, 1)
                dve.wait_ge(s_bias, 1)
                dve.tensor_tensor(gate_bias[:, :], bias_ih, bias_hh, ALU.add).then_inc(s_bias, 1)
                dve.tensor_scalar(neg_scale[:, :], back_scale[:, Z:Z + 1], -1.0, None, ALU.mult).then_inc(s_const, 1)
                dve.tensor_scalar(bhn_scaled[:, :], bias_hh[:, NN:NN + 1], w_scale[:, NN:NN + 1], W_TOP * H_SCALE,
                                  ALU.mult, ALU.mult).then_inc(s_const, 1)
                dve.wait_ge(s_bias, 2)
                dve.tensor_scalar(gate_bias[:, Z:Z + 1], gate_bias[:, Z:Z + 1], -1.0, None, ALU.mult).then_inc(s_const, 1)
                dve.wait_ge(s_const, 3)

            def adjacency(group):
                dve.tensor_scalar(adj_one[:, group_columns(group)], adj_int[:, group_columns(group)], 0.0, None,
                                  ALU.not_equal).then_inc(s_one, 1)

            def norm_stats(group, ab):
                for b in range(GPG):
                    dve.bn_stats(stats[:, ab, b, :], x_all[:, bass.ds(group * N + b * P, P)]).then_inc(s_bn, 1)
                dve.wait_ge(s_bn, (group + 1) * GPG)
                adjacency(group)
                for b in range(GPG):
                    dve.bn_aggr(moments[:, ab, b, :], stats[:, ab, b, :]).then_inc(s_mom, 1)
                dve.wait_ge(s_mom, (group + 1) * GPG)
                dve.tensor_scalar(var_eps[:, ab, :], moments[:, ab, :, 1], EPS, H_SCALE ** -2,
                                  ALU.add, ALU.mult).then_inc(s_var, 1)

            def normalise(group, ab):
                dve.wait_ge(s_inv, group + 1)
                for b in range(GPG):
                    dve.tensor_scalar(normed[:, ab, b * P:(b + 1) * P], x_all[:, bass.ds(group * N + b * P, P)],
                                      moments[:, ab, b, 0:1], inv_std[:, ab, b:b + 1],
                                      ALU.subtract, ALU.mult).then_inc(s_normed, 1)

            def split_normed(group, ab):
                dve.wait_ge(s_normed, (group + 1) * GPG)
                dve.tensor_scalar(nodes16[:, 0, ab, 0, :], normed[:, ab, :], 0.0, None, ALU.max).then_inc(s_hi0, 1)
                dve.wait_ge(s_hi0, group + 1)
                dve.scalar_tensor_tensor(out=nodes16[:, 0, ab, 1, :], in0=normed[:, ab, :], scalar=0.0,
                                         in1=nodes16[:, 0, ab, 0, :], op0=ALU.max,
                                         op1=ALU.subtract).then_inc(s_nodes0, 1)

            def u_lo(it):
                dve.wait_ge(s_uhi, it.n + 1)
                dve.scalar_tensor_tensor(out=u16[:, 1, :], in0=ps_u[:, :], scalar=U_SCALE, in1=u16[:, 0, :],
                                         op0=ALU.mult, op1=ALU.subtract).then_inc(s_ulo, 1)

            def n_sum(it):
                dve.wait_ge(s_r, it.n + 1)
                dve.scalar_tensor_tensor(out=rn_sb[:, :], in0=ps_hn[:, :], scalar=bhn_scaled[:, :], in1=r_sb[:, :],
                                         op0=ALU.add, op1=ALU.mult).then_inc(s_rn, 1)
                dve.wait_ge(s_rn, it.n + 1)
                dve.wait_ge(s_pn, it.n + 1)
                bank = ps_in[parity(it)]
                dve.tensor_tensor(bank[:, :], bank[:, :], rn_sb[:, :], ALU.add).then_inc(s_nsum, 1)

            def difference(it):
                if it.layer == 1:
                    dve.wait_ge(s_state0, it.group + 1)
                wait_before(dve, s_step, it.n - 1)
                dve.wait_ge(s_tanh, it.n + 1)
                dve.scalar_tensor_tensor(out=diff[:, parity(it), :], in0=ps_in[parity(it)][:, :], scalar=H_SCALE,
                                         in1=state[:, it.layer - 1, it.ab, :], op0=ALU.mult,
                                         op1=ALU.subtract).then_inc(s_diff, 1)

            def state_lo(it):
                dve.wait_ge(s_hi, it.n + 1)
                dve.tensor_tensor(state16[:, it.layer, it.ab, 1, :], state[:, it.layer, it.ab, :],
                                  state16[:, it.layer, it.ab, 0, :], ALU.subtract).then_inc(s_lo, 1)

            def result(it):
                dve.wait_ge(s_turn, it.n + 1)
                cols = group_columns(it.group)
                dve.tensor_tensor(x_all[:, cols], ps_turn[:, :], x_all[:, cols], ALU.add).then_inc(s_taken[LAYERS], 1)

            def slot(t, k):
                for st in slot_steps(t, k, pairs):
                    if st.item is not None:
                        _, b1, b2, b3 = st.back
                        if b1 is not None:
                            n_sum(b1)
                        if st.early:
                            if b3 is not None and not st.early_before and b3.layer == LAYERS:
                                result(b3)
                            state_lo(b2)
                            if b2.layer == LAYERS:
                                result(b2)
                        u_lo(st.item)
                        if not st.early and b2 is not None:
                            state_lo(b2)
                        if b1 is not None:
                            difference(b1)
                        if not st.early and b3 is not None and not st.early_before and b3.layer == LAYERS:
                            result(b3)
                    if st.pos in (0, 1) and 0 <= t - 1 < pairs:
                        split_normed(2 * (k - 1) + st.pos, st.pos)
                    if t < pairs and st.pos in (2, 3):
                        if st.pos == 2:
                            dve.wait_ge(s_x, (k + 1) * 16)
                            dve.wait_ge(s_adj, (k + 1) * 16)
                        norm_stats(2 * k + st.pos - 2, st.pos - 2)
                    if t < pairs and st.pos in (4, 5):
                        normalise(2 * k + st.pos - 4, st.pos - 4)
                if t == 0:
                    setup_weights()

            setup()
            slots(dve, slot)
            for st in drain_steps(last_slot, pairs):
                _, b1, b2, b3 = st.back
                if b1 is not None:
                    n_sum(b1)
                    difference(b1)
                if b2 is not None:
                    state_lo(b2)
                    result(b2)

        @block.gpsimd
        def _(pool):
            def setup():
                pool.memset(ident[:, :], 0.0).then_inc(s_zero, 1)
                pool.wait_ge(s_zero, 1)
                pool.affine_select(out=ident[:, :], in_=ident[:, :], compare_op=ALU.not_equal, fill=1.0, base=0,
                                   pattern=[[-1, P]], channel_multiplier=1).then_inc(s_ident, 1)

            def inverse_std(group, ab):
                pool.wait_ge(s_var, group + 1)
                pool.tensor_tensor(inv_std[:, ab, :], var_eps[:, ab, :], half_neg[:, :], ALU.pow).then_inc(s_inv, 1)

            def new_state(it):
                l, ab = it.layer, it.ab
                pool.wait_ge(s_diff, it.n + 1)
                pool.wait_ge(s_z, it.n + 1)
                wait_before(pool, s_state, it.n)
                pool.tensor_tensor(step_sb[:, :], diff[:, parity(it), :], z_sb[:, parity(it), :],
                                   ALU.mult).then_inc(s_step, 1)
                pool.wait_ge(s_step, it.n + 1)
                pool.tensor_tensor(state[:, l, ab, :], state[:, l - 1, ab, :], step_sb[:, :],
                                   ALU.add).then_inc(s_state, 1)

            def state_normed(group, ab):
                pool.wait_ge(s_state16_0, group + 1)
                pool.tensor_tensor(state[:, 0, ab, :], state16[:, 0, ab, 0, :], state16[:, 0, ab, 1, :],
                                   ALU.add).then_inc(s_state0, 1)

            def slot(t, k):
                for st in slot_steps(t, k, pairs):
                    if st.item is not None and st.back[1] is not None:
                        new_state(st.back[1])
                    if st.pos in (2, 3) and 0 <= t - 1 < pairs:
                        state_normed(2 * (k - 1) + st.pos - 2, st.pos - 2)
                    if st.pos in (3, 4) and t < pairs:
                        inverse_std(2 * k + st.pos - 3, st.pos - 3)

            setup()
            pool.wait_ge(s_ident16, 1)
            slots(pool, slot)
            for st in drain_steps(last_slot, pairs):
                if st.back[1] is not None:
                    new_state(st.back[1])


def parity(it):
    return it.ab


def kernel(**inputs):
    import numpy as np
    from concourse import bacc
    from concourse.bass_utils import run_bass_kernel_spmd

    nc = bacc.Bacc("TRN2", target_bir_lowering=False, num_devices=1)
    names = ["x", "adj", "L0_gnn_weight", "L0_gnn_w_ih", "L0_gnn_w_hh", "L0_gnn_b_ih", "L0_gnn_b_hh"]
    arrays, args = {}, []
    for name in names:
        a = np.ascontiguousarray(inputs[name])
        arrays[f"in_{name}"] = a
        args.append(nc.dram_tensor(f"in_{name}", a.shape, mybir.dt.from_np(a.dtype), kind="ExternalInput").ap())
    shape = inputs["x"].shape
    args.append(nc.dram_tensor("out_h", shape, F32, kind="ExternalOutput").ap())
    build(nc, *args)
    done = run_bass_kernel_spmd(nc, [arrays], core_ids=[0])
    return done.results[0]["out_h"]
```

```python
from contextlib import ExitStack

import concourse.bass as bass
from concourse import mybir

F32 = mybir.dt.float32
F16 = mybir.dt.float16
I32 = mybir.dt.int32
ALU = mybir.AluOpType
ACT = mybir.ActivationFunctionType
AX_X = mybir.AxisListType.X

P = 128
GPG = 4
N = GPG * P
LAYERS = 3
R, Z, NN = range(3)
GATES = 3
WHH = LAYERS
SLOTS_W = LAYERS + 1
EPS = 1e-5
H_SCALE = 2.0 ** 11
U_SCALE = 2.0 ** -6
W_TOP = 2.0 ** 13
EXPONENT_BITS = 0x7F800000

BATCH = 4
ITEMS = LAYERS * BATCH
LAG = 3
STATS_AT = {3: 0, 5: 1, 8: 2, 11: 3}
NORM_AT = {4: 0, 6: 1, 9: 2, 12: 3}
SPLIT_AT = {5: 0, 7: 1, 10: 2, 13: 3}
TURN0_AT = {6: 0, 8: 1, 11: 2, 14: 3}


class Item:

    def __init__(self, q, m):
        self.n = q * ITEMS + m
        self.layer = m % ITEMS // BATCH + 1
        self.j = m % BATCH
        self.group = (q + m // ITEMS) * BATCH + self.j
        self.parity = m % 2


class Step:

    def __init__(self, q, m, first=0, last=None):
        def item(i):
            return Item(q, i) if i >= first and (last is None or i <= last) else None

        self.m = m
        self.item = item(m)
        self.back = [item(m - i) for i in range(LAG + 1)]
        self.turned_before = item(m - LAG - 1)


def build(nc, x, adj, weight, w_ih, w_hh, b_ih, b_hh, out):
    graphs = x.shape[0]
    groups = graphs // GPG
    batches = groups // BATCH

    with ExitStack() as ctx:
        def sb(name, shape, dt):
            return ctx.enter_context(nc.sbuf_tensor(name, shape, dt))

        def psum(name):
            return ctx.enter_context(nc.psum_tensor(name, [P, N], F32))

        def sem(name):
            return ctx.enter_context(nc.semaphore(name))

        ps_r, ps_z, ps_hn = psum("ps_r"), psum("ps_z"), psum("ps_hn")
        ps_in = [psum("ps_in0"), psum("ps_in1")]
        ps_u, ps_turn, ps_turn0 = psum("ps_u"), psum("ps_turn"), psum("ps_turn0")

        def halves(bank):
            return bank[:, :].bitcast(F16).rearrange("p (c n) -> p c n", c=2)

        x_all = sb("x_all", [P, graphs * P], F32)
        adj_int = sb("adj_int", [P, graphs * P], I32)
        adj_one = sb("adj_one", [P, graphs * P], F16)
        ident = sb("ident", [P, P], F32)
        ident16 = sb("ident16", [P, P], F16)
        ident_out = sb("ident_out", [P, P], F16)
        wih_rows = sb("wih_rows", [P, GATES, P], F32)
        wl_rows = sb("wl_rows", [P, LAYERS, P], F32)
        wih_t = sb("wih_t", [P, GATES, P], F32)
        wl_t = sb("wl_t", [P, LAYERS, P], F32)
        w_rows = sb("w_rows", [P, GATES, SLOTS_W, P], F32)
        w_hi = sb("w_hi", [P, GATES, SLOTS_W, P], F16)
        w_lo = sb("w_lo", [P, GATES, SLOTS_W, P], F16)
        bias_rows = sb("bias_rows", [2 * GATES, P], F32)
        biases = sb("biases", [P, 2 * GATES], F32)
        bias_ih, bias_hh = biases[:, 0:GATES], biases[:, GATES:2 * GATES]
        w_top = sb("w_top", [P, GATES], F32)
        w_scale = sb("w_scale", [P, GATES], F32)
        back_scale = sb("back_scale", [P, GATES], F32)
        gate_bias = sb("gate_bias", [P, GATES], F32)
        neg_scale = sb("neg_scale", [P, 1], F32)
        bhn_scaled = sb("bhn_scaled", [P, 1], F32)
        half_neg = sb("half_neg", [P, GPG], F32)
        stats = sb("stats", [P, BATCH, GPG, 6], F32)
        moments = sb("moments", [P, BATCH, GPG, 2], F32)
        var_eps = sb("var_eps", [P, BATCH, GPG], F32)
        inv_std = sb("inv_std", [P, BATCH, GPG], F32)
        normed = sb("normed", [P, BATCH, N], F32)
        state = sb("state", [P, 2, BATCH, N], F32)
        state16 = sb("state16", [P, 2, BATCH, 2, N], F16)
        nodes16 = sb("nodes16", [P, 2, BATCH, 2, N], F16)
        u16 = sb("u16", [P, 2, N], F16)
        r_sb = sb("r_sb", [P, N], F32)
        z_sb = sb("z_sb", [P, 2, N], F32)
        rn_sb = sb("rn_sb", [P, N], F32)
        diff = sb("diff", [P, 2, N], F32)
        step_sb = sb("step_sb", [P, N], F32)

        s_w, s_x, s_adj, s_store = sem("s_w"), sem("s_x"), sem("s_adj"), sem("s_store")
        s_x_first = [sem(f"s_x_first{j}") for j in range(BATCH)]
        s_adj_first = [sem(f"s_adj_first{j}") for j in range(BATCH)]
        s_zero, s_ident, s_ident16, s_scale, s_bias = (
            sem("s_zero"), sem("s_ident"), sem("s_ident16"), sem("s_scale"), sem("s_bias"))
        s_wt, s_wt_sb, s_prod = sem("s_wt"), sem("s_wt_sb"), sem("s_prod")
        s_rows, s_const, s_wturn, s_whi, s_wlo = (
            sem("s_rows"), sem("s_const"), sem("s_wturn"), sem("s_whi"), sem("s_wlo"))
        s_bn, s_mom, s_var, s_inv, s_normed, s_one = (
            sem("s_bn"), sem("s_mom"), sem("s_var"), sem("s_inv"), sem("s_normed"), sem("s_one"))
        s_hi0, s_nodes0, s_turn0, s_state16_0, s_state0 = (
            sem("s_hi0"), sem("s_nodes0"), sem("s_turn0"), sem("s_state16_0"), sem("s_state0"))
        s_agg, s_uhi, s_ulo = sem("s_agg"), sem("s_uhi"), sem("s_ulo")
        s_pr, s_pn, s_pz = sem("s_pr"), sem("s_pn"), sem("s_pz")
        s_r, s_z, s_rn, s_nsum, s_tanh = sem("s_r"), sem("s_z"), sem("s_rn"), sem("s_nsum"), sem("s_tanh")
        s_diff, s_step, s_state, s_hi, s_lo = (
            sem("s_diff"), sem("s_step"), sem("s_state"), sem("s_hi"), sem("s_lo"))
        s_turn = sem("s_turn")
        s_taken = [None] + [sem(f"s_taken{l}") for l in range(1, LAYERS + 1)]

        block = ctx.enter_context(nc.Block())

        def wait_before(eng, s, value):
            if isinstance(value, int) and value <= 0:
                return
            eng.wait_ge(s, value)

        def run(eng, step):
            for m in range(LAG):
                step(Step(0, m), 0, False)
            with eng.Fori(0, batches - 1) as q:
                for m in range(LAG, ITEMS + LAG):
                    step(Step(q, m), q, True)
            for m in range(LAG, ITEMS + LAG):
                step(Step(batches - 1, m, last=ITEMS - 1), batches - 1, False)

        def group_columns(group):
            return bass.ds(group * N, N)

        @block.sync
        def _(sp):
            x_src = x.rearrange("g n d -> n g d")
            adj_src = adj.rearrange("g s t -> s g t")
            out_dst = out.rearrange("g n d -> n g d")
            for j in range(BATCH):
                cols, src = slice(j * N, (j + 1) * N), slice(j * GPG, (j + 1) * GPG)
                sp.dma_start(x_all[:, cols].rearrange("p (g d) -> p g d", d=P), x_src[:, src, :]).then_inc(s_x_first[j], 16)
                if j == 0:
                    sp.dma_start(wih_rows[:, :, :], w_ih.rearrange("(g e) f -> e g f", e=P)).then_inc(s_w, 16)
                    sp.dma_start(wl_rows[:, :, :], weight.rearrange("l d f -> d l f")).then_inc(s_w, 16)
                    sp.dma_start(bias_rows[0:GATES, :], b_ih.rearrange("(g e) -> g e", e=P)).then_inc(s_w, 16)
                    sp.dma_start(bias_rows[GATES:2 * GATES, :], b_hh.rearrange("(g e) -> g e", e=P)).then_inc(s_w, 16)
                    sp.dma_start(w_rows[:, :, WHH, :], w_hh.rearrange("(g e) f -> e g f", e=P)).then_inc(s_w, 16)
                sp.dma_start(adj_int[:, cols].rearrange("p (g d) -> p g d", d=P), adj_src[:, src, :]).then_inc(s_adj_first[j], 16)
            first_pair = BATCH // 2

            def load(pair):
                first = pair * (2 * GPG) if isinstance(pair, int) else sp.snap(pair * (2 * GPG))
                cols, src = bass.ds(first * P, 2 * N), bass.ds(first, 2 * GPG)
                if not isinstance(pair, int):
                    sp.wait_ge(s_x, (pair - first_pair) * 16)
                    sp.wait_ge(s_adj, (pair - first_pair) * 16)
                sp.dma_start(x_all[:, cols].rearrange("p (g d) -> p g d", d=P), x_src[:, src, :]).then_inc(s_x, 16)
                sp.dma_start(adj_int[:, cols].rearrange("p (g d) -> p g d", d=P), adj_src[:, src, :]).then_inc(s_adj, 16)

            load(first_pair)
            with sp.Fori(first_pair + 1, groups // 2) as pair:
                load(pair)
            with sp.Fori(0, groups) as g:
                sp.wait_ge(s_taken[LAYERS], g + 1)
                sp.dma_start(out_dst[:, bass.ds(g * GPG, GPG), :],
                             x_all[:, group_columns(g)].rearrange("p (g d) -> p g d", d=P)).then_inc(s_store, 16)
            sp.wait_ge(s_store, groups * 16)

        def source(it):
            return 0 if it.layer == 1 else 1

        @block.tensor
        def _(pe):
            def product(bank, gate, slot, hi, lo, first, last):
                wh, wl = w_hi[:, gate, slot, :], w_lo[:, gate, slot, :]
                pe.matmul(bank[:, :], wh, hi, start=first, stop=False)
                pe.matmul(bank[:, :], wh, lo, start=False, stop=False)
                return pe.matmul(bank[:, :], wl, hi, start=False, stop=last)

            def setup():
                pe.wait_ge(s_ident, 1)
                pe.wait_ge(s_w, 5 * 16)
                for l in range(LAYERS):
                    pe.transpose(ps_z[:, l * P:(l + 1) * P], wl_rows[:, l, :], ident[:, :])
                m = pe.transpose(ps_u[:, 0:2 * GATES], bias_rows[:, :], ident[0:2 * GATES, 0:2 * GATES])
                m.then_inc(s_wt, 1)
                for g in range(GATES):
                    m = pe.transpose(ps_r[:, g * P:(g + 1) * P], wih_rows[:, g, :], ident[:, :])
                m.then_inc(s_wt, 1)
                pe.wait_ge(s_wt_sb, 2)
                for g, bank in enumerate((ps_hn, ps_in[0], ps_in[1])):
                    pe.matmul(bank[:, 0:LAYERS * P], wih_t[:, g, :], wl_t[:, :, :].rearrange("p l d -> p (l d)"),
                              start=True, stop=True).then_inc(s_prod, 1)
                pe.wait_ge(s_bias, 1)
                for g, bank in enumerate((ps_r, ps_z, ps_u)):
                    pe.wait_ge(s_rows, GATES + 1 + g)
                    for s in range(SLOTS_W):
                        m = pe.transpose(bank[:, s * P:(s + 1) * P], w_rows[:, g, s, :], ident[:, :])
                    m.then_inc(s_wturn, 1)
                pe.wait_ge(s_wlo, GATES)
                pe.wait_ge(s_ident16, 3)

            def aggregate(it):
                if it.layer == 1:
                    pe.wait_ge(s_nodes0, it.group + 1)
                    pe.wait_ge(s_one, it.group + 1)
                else:
                    pe.wait_ge(s_taken[it.layer - 1], it.group + 1)
                wait_before(pe, s_ulo, it.n)
                for b in range(GPG):
                    cols = slice(b * P, (b + 1) * P)
                    a = adj_one[:, bass.ds(it.group * N + b * P, P)]
                    pe.matmul(ps_u[:, cols], nodes16[:, source(it), it.j, 0, cols], a, start=True, stop=False)
                    m = pe.matmul(ps_u[:, cols], nodes16[:, source(it), it.j, 1, cols], a, start=False, stop=True)
                m.then_inc(s_agg, 1)

            def hidden_part_r(it):
                hi, lo = (state16[:, source(it), it.j, c, :] for c in (0, 1))
                if it.layer == 1:
                    pe.wait_ge(s_state16_0, it.group + 1)
                wait_before(pe, s_r, it.n)
                product(ps_r, R, WHH, hi, lo, True, False)

            def hidden_part(it):
                hi, lo = (state16[:, source(it), it.j, c, :] for c in (0, 1))
                wait_before(pe, s_z, it.n)
                product(ps_z, Z, WHH, hi, lo, True, False)
                wait_before(pe, s_rn, it.n)
                product(ps_hn, NN, WHH, hi, lo, True, True)

            def input_part(it):
                hi, lo, s = u16[:, 0, :], u16[:, 1, :], it.layer - 1
                pe.wait_ge(s_ulo, it.n + 1)
                product(ps_r, R, s, hi, lo, False, True).then_inc(s_pr, 1)
                wait_before(pe, s_diff, it.n - 1)
                product(ps_in[it.parity], NN, s, hi, lo, True, True).then_inc(s_pn, 1)
                product(ps_z, Z, s, hi, lo, False, True).then_inc(s_pz, 1)

            def turn(it, st):
                pe.wait_ge(s_lo, it.n + 1)
                before = st.turned_before
                if before is not None:
                    pe.wait_ge(s_taken[before.layer], before.group + 1)
                else:
                    pe.wait_ge(s_rn, st.item.n)
                for b in range(GPG):
                    cols = slice(b * P, (b + 1) * P)
                    for c in (0, 1):
                        part = state16[:, 1, it.j, c, cols]
                        if it.layer < LAYERS:
                            m = pe.transpose(halves(ps_turn)[:, c, cols], part, ident16[:, :])
                        else:
                            m = pe.matmul(ps_turn[:, cols], part, ident_out[:, :], start=(c == 0), stop=(c == 1))
                m.then_inc(s_turn, 1)

            def turn_normed(group, j):
                pe.wait_ge(s_nodes0, group + 1)
                wait_before(pe, s_state16_0, group)
                for b in range(GPG):
                    cols = slice(b * P, (b + 1) * P)
                    for c in (0, 1):
                        m = pe.transpose(halves(ps_turn0)[:, c, cols], nodes16[:, 0, j, c, cols], ident16[:, :])
                m.then_inc(s_turn0, 1)

            def step(st, q, prepare):
                it, b3 = st.item, st.back[3]
                if it is not None:
                    aggregate(it)
                    hidden_part_r(it)
                if b3 is not None:
                    turn(b3, st)
                if it is not None:
                    hidden_part(it)
                if prepare and st.m in TURN0_AT:
                    turn_normed((q + 1) * BATCH + TURN0_AT[st.m], TURN0_AT[st.m])
                elif isinstance(q, int) and q == 0 and st.m < LAG:
                    turn_normed(st.m + 1, st.m + 1)
                if it is not None:
                    input_part(it)

            setup()
            turn_normed(0, 0)
            run(pe, step)

        @block.scalar
        def _(act):
            def setup():
                act.wait_ge(s_ident16, 1)
                act.activation(r_sb[:, 0:1], half_neg[:, 0:1], ACT.Sigmoid)
                act.wait_ge(s_wt, 2)
                act.activation(wih_t[:, :, :].rearrange("p g e -> p (g e)"), ps_r[:, 0:GATES * P],
                               ACT.Copy).then_inc(s_wt_sb, 1)
                for g, bank in enumerate((ps_hn, ps_in[0], ps_in[1])):
                    act.wait_ge(s_prod, g + 1)
                    act.activation(w_rows[:, g, 0:LAYERS, :].rearrange("p l d -> p (l d)"), bank[:, 0:LAYERS * P],
                                   ACT.Copy, scale=1.0 / U_SCALE).then_inc(s_rows, 1)
                for g, bank in enumerate((ps_r, ps_z, ps_u)):
                    act.wait_ge(s_wturn, g + 1)
                    act.activation(w_hi[:, g, :, :].rearrange("p s e -> p (s e)"), bank[:, :],
                                   ACT.Copy).then_inc(s_whi, 1)
                act.wait_ge(s_const, 3)

            def gate_z(it):
                act.wait_ge(s_pz, it.n + 1)
                wait_before(act, s_step, it.n - 1)
                act.activation(z_sb[:, it.parity, :], ps_z[:, :], ACT.Sigmoid,
                               bias=gate_bias[:, Z:Z + 1], scale=neg_scale[:, :]).then_inc(s_z, 1)

            def gate_r(it):
                act.wait_ge(s_pr, it.n + 1)
                wait_before(act, s_rn, it.n)
                act.activation(r_sb[:, :], ps_r[:, :], ACT.Sigmoid,
                               bias=gate_bias[:, R:R + 1], scale=back_scale[:, R:R + 1]).then_inc(s_r, 1)

            def gate_n(it):
                act.wait_ge(s_nsum, it.n + 1)
                bank = ps_in[it.parity]
                act.activation(bank[:, :], bank[:, :], ACT.Tanh,
                               bias=biases[:, NN:NN + 1], scale=back_scale[:, NN:NN + 1]).then_inc(s_tanh, 1)

            def u_hi(it):
                act.wait_ge(s_agg, it.n + 1)
                act.activation(u16[:, 0, :], ps_u[:, :], ACT.Copy, scale=U_SCALE).then_inc(s_uhi, 1)

            def state_hi(it):
                act.wait_ge(s_state, it.n + 1)
                act.activation(state16[:, 1, it.j, 0, :], state[:, 1, it.j, :], ACT.Copy).then_inc(s_hi, 1)

            def take_turned(it):
                act.wait_ge(s_turn, it.n + 1)
                act.activation(nodes16[:, 1, it.j, :, :].rearrange("p c n -> p (c n)"),
                               ps_turn[:, :].bitcast(F16), ACT.Copy).then_inc(s_taken[it.layer], 1)

            def take_normed(group, j):
                act.wait_ge(s_turn0, group + 1)
                act.activation(state16[:, 0, j, :, :].rearrange("p c n -> p (c n)"),
                               ps_turn0[:, :].bitcast(F16), ACT.Copy).then_inc(s_state16_0, 1)

            def normed_hi(group, j):
                act.wait_ge(s_normed, (group + 1) * GPG)
                act.activation(nodes16[:, 0, j, 0, :], normed[:, j, :], ACT.Relu).then_inc(s_hi0, 1)

            def step(st, q, prepare):
                it, b1, b2, b3 = st.back
                if b1 is not None:
                    gate_z(b1)
                if it is not None:
                    u_hi(it)
                if prepare and st.m in SPLIT_AT:
                    normed_hi((q + 1) * BATCH + SPLIT_AT[st.m], SPLIT_AT[st.m])
                if b2 is not None:
                    state_hi(b2)
                if b1 is not None:
                    gate_n(b1)
                if b3 is not None and b3.layer < LAYERS:
                    take_turned(b3)
                if it is not None:
                    gate_r(it)
                if prepare and st.m in TURN0_AT:
                    take_normed((q + 1) * BATCH + TURN0_AT[st.m], TURN0_AT[st.m])
                elif isinstance(q, int) and q == 0 and st.m < LAG:
                    take_normed(st.m + 1, st.m + 1)
                    if st.m + 2 < BATCH:
                        normed_hi(st.m + 2, st.m + 2)

            setup()
            normed_hi(0, 0)
            take_normed(0, 0)
            normed_hi(1, 1)
            run(act, step)

        @block.vector
        def _(dve):
            def setup():
                dve.memset(half_neg[:, :], -0.5).then_inc(s_ident16, 1)
                dve.wait_ge(s_ident, 1)
                dve.tensor_copy(ident16[:, :], ident[:, :]).then_inc(s_ident16, 1)
                dve.tensor_scalar(ident_out[:, :], ident[:, :], 1.0 / H_SCALE, None, ALU.mult).then_inc(s_ident16, 1)

            def turn_weights():
                dve.wait_ge(s_wt, 1)
                dve.tensor_copy(wl_t[:, :, :].rearrange("p l d -> p (l d)"), ps_z[:, 0:LAYERS * P]).then_inc(s_wt_sb, 1)
                dve.tensor_copy(biases[:, :], ps_u[:, 0:2 * GATES]).then_inc(s_bias, 1)

            def scale_weights():
                for g in range(GATES):
                    dve.wait_ge(s_rows, g + 1)
                    dve.tensor_reduce(w_top[:, g:g + 1], w_rows[:, g, :, :].rearrange("p s d -> p (s d)"),
                                      AX_X, ALU.max, apply_absolute_value=True).then_inc(s_scale, 1)
                dve.wait_ge(s_scale, GATES)
                dve.tensor_scalar(w_top[:, :], w_top[:, :], 2.0 ** -60, 2.0 ** 60, ALU.max, ALU.min).then_inc(s_scale, 1)
                dve.wait_ge(s_scale, GATES + 1)
                top_bits = w_top[:, :].bitcast(I32)
                dve.tensor_scalar(top_bits, top_bits, EXPONENT_BITS, None, ALU.bitwise_and).then_inc(s_scale, 1)
                dve.wait_ge(s_scale, GATES + 2)
                dve.reciprocal(w_scale[:, :], w_top[:, :]).then_inc(s_scale, 1)
                dve.tensor_scalar(back_scale[:, :], w_top[:, :], 1.0 / (W_TOP * H_SCALE), None, ALU.mult).then_inc(s_scale, 1)
                dve.wait_ge(s_scale, GATES + 4)
                for g in range(GATES):
                    rows = w_rows[:, g, :, :].rearrange("p s d -> p (s d)")
                    dve.tensor_scalar(rows, rows, w_scale[:, g:g + 1], W_TOP, ALU.mult, ALU.mult).then_inc(s_rows, 1)
                dve.wait_ge(s_bias, 1)
                dve.tensor_tensor(gate_bias[:, :], bias_ih, bias_hh, ALU.add).then_inc(s_bias, 1)
                dve.tensor_scalar(neg_scale[:, :], back_scale[:, Z:Z + 1], -1.0, None, ALU.mult).then_inc(s_const, 1)
                dve.tensor_scalar(bhn_scaled[:, :], bias_hh[:, NN:NN + 1], w_scale[:, NN:NN + 1], W_TOP * H_SCALE,
                                  ALU.mult, ALU.mult).then_inc(s_const, 1)
                dve.wait_ge(s_bias, 2)
                dve.tensor_scalar(gate_bias[:, Z:Z + 1], gate_bias[:, Z:Z + 1], -1.0, None, ALU.mult).then_inc(s_const, 1)
                dve.wait_ge(s_const, 3)

            def split_weights():
                for g, bank in enumerate((ps_r, ps_z, ps_u)):
                    dve.wait_ge(s_whi, g + 1)
                    dve.tensor_tensor(w_lo[:, g, :, :].rearrange("p s e -> p (s e)"), bank[:, :],
                                      w_hi[:, g, :, :].rearrange("p s e -> p (s e)"), ALU.subtract).then_inc(s_wlo, 1)

            def adjacency(group):
                dve.tensor_scalar(adj_one[:, group_columns(group)], adj_int[:, group_columns(group)], 0.0, None,
                                  ALU.not_equal).then_inc(s_one, 1)

            def norm_stats(group, j):
                for b in range(GPG):
                    dve.bn_stats(stats[:, j, b, :], x_all[:, bass.ds(group * N + b * P, P)]).then_inc(s_bn, 1)

            def norm_moments(group, j):
                dve.wait_ge(s_bn, (group + 1) * GPG)
                adjacency(group)
                for b in range(GPG):
                    dve.bn_aggr(moments[:, j, b, :], stats[:, j, b, :]).then_inc(s_mom, 1)
                dve.wait_ge(s_mom, (group + 1) * GPG)
                dve.tensor_scalar(var_eps[:, j, :], moments[:, j, :, 1], EPS, H_SCALE ** -2,
                                  ALU.add, ALU.mult).then_inc(s_var, 1)

            def normalise(group, j):
                dve.wait_ge(s_inv, group + 1)
                for b in range(GPG):
                    dve.tensor_scalar(normed[:, j, b * P:(b + 1) * P], x_all[:, bass.ds(group * N + b * P, P)],
                                      moments[:, j, b, 0:1], inv_std[:, j, b:b + 1],
                                      ALU.subtract, ALU.mult).then_inc(s_normed, 1)

            def normed_lo(group, j):
                dve.wait_ge(s_hi0, group + 1)
                dve.scalar_tensor_tensor(out=nodes16[:, 0, j, 1, :], in0=normed[:, j, :], scalar=0.0,
                                         in1=nodes16[:, 0, j, 0, :], op0=ALU.max,
                                         op1=ALU.subtract).then_inc(s_nodes0, 1)

            def u_lo(it):
                dve.wait_ge(s_uhi, it.n + 1)
                dve.scalar_tensor_tensor(out=u16[:, 1, :], in0=ps_u[:, :], scalar=U_SCALE, in1=u16[:, 0, :],
                                         op0=ALU.mult, op1=ALU.subtract).then_inc(s_ulo, 1)

            def reset_part(it):
                dve.wait_ge(s_r, it.n + 1)
                dve.scalar_tensor_tensor(out=rn_sb[:, :], in0=ps_hn[:, :], scalar=bhn_scaled[:, :], in1=r_sb[:, :],
                                         op0=ALU.add, op1=ALU.mult).then_inc(s_rn, 1)

            def n_sum(it):
                dve.wait_ge(s_rn, it.n + 1)
                dve.wait_ge(s_pn, it.n + 1)
                bank = ps_in[it.parity]
                dve.tensor_tensor(bank[:, :], bank[:, :], rn_sb[:, :], ALU.add).then_inc(s_nsum, 1)

            def difference(it):
                if it.layer == 1:
                    dve.wait_ge(s_state0, it.group + 1)
                wait_before(dve, s_step, it.n - 1)
                dve.wait_ge(s_tanh, it.n + 1)
                dve.scalar_tensor_tensor(out=diff[:, it.parity, :], in0=ps_in[it.parity][:, :], scalar=H_SCALE,
                                         in1=state[:, source(it), it.j, :], op0=ALU.mult,
                                         op1=ALU.subtract).then_inc(s_diff, 1)

            def result(it):
                dve.wait_ge(s_turn, it.n + 1)
                cols = group_columns(it.group)
                dve.tensor_tensor(x_all[:, cols], ps_turn[:, :], x_all[:, cols], ALU.add).then_inc(s_taken[LAYERS], 1)

            def prepare_first(j):
                dve.wait_ge(s_x_first[j], 16)
                dve.wait_ge(s_adj_first[j], 16)
                norm_stats(j, j)
                norm_moments(j, j)

            def step(st, q, prepare):
                it, b1, b2, b3 = st.back
                if b1 is not None:
                    reset_part(b1)
                if it is not None:
                    u_lo(it)
                if b1 is not None:
                    n_sum(b1)
                if b3 is not None and b3.layer == LAYERS:
                    result(b3)
                if prepare:
                    if st.m in STATS_AT:
                        loads = (q + 1) * (BATCH // 2)
                        dve.wait_ge(s_x, loads * 16)
                        dve.wait_ge(s_adj, loads * 16)
                        norm_stats((q + 1) * BATCH + STATS_AT[st.m], STATS_AT[st.m])
                    if st.m in NORM_AT:
                        normalise((q + 1) * BATCH + NORM_AT[st.m], NORM_AT[st.m])
                    if st.m in SPLIT_AT:
                        normed_lo((q + 1) * BATCH + SPLIT_AT[st.m], SPLIT_AT[st.m])
                if b1 is not None:
                    difference(b1)
                if prepare:
                    if st.m in STATS_AT:
                        norm_moments((q + 1) * BATCH + STATS_AT[st.m], STATS_AT[st.m])
                elif isinstance(q, int) and q == 0 and st.m + 2 < BATCH:
                    prepare_first(st.m + 2)
                    normalise(st.m + 2, st.m + 2)
                    normed_lo(st.m + 2, st.m + 2)

            setup()
            prepare_first(0)
            turn_weights()
            normalise(0, 0)
            prepare_first(1)
            scale_weights()
            normalise(1, 1)
            split_weights()
            normed_lo(0, 0)
            normed_lo(1, 1)
            run(dve, step)

        @block.gpsimd
        def _(pool):
            def setup():
                pool.memset(ident[:, :], 0.0).then_inc(s_zero, 1)
                pool.wait_ge(s_zero, 1)
                pool.affine_select(out=ident[:, :], in_=ident[:, :], compare_op=ALU.not_equal, fill=1.0, base=0,
                                   pattern=[[-1, P]], channel_multiplier=1).then_inc(s_ident, 1)
                pool.wait_ge(s_ident16, 1)

            def inverse_std(group, j):
                pool.wait_ge(s_var, group + 1)
                pool.tensor_tensor(inv_std[:, j, :], var_eps[:, j, :], half_neg[:, :], ALU.pow).then_inc(s_inv, 1)

            def new_state(it):
                pool.wait_ge(s_diff, it.n + 1)
                pool.wait_ge(s_z, it.n + 1)
                wait_before(pool, s_state, it.n)
                pool.tensor_tensor(step_sb[:, :], diff[:, it.parity, :], z_sb[:, it.parity, :],
                                   ALU.mult).then_inc(s_step, 1)
                pool.wait_ge(s_step, it.n + 1)
                pool.tensor_tensor(state[:, 1, it.j, :], state[:, source(it), it.j, :], step_sb[:, :],
                                   ALU.add).then_inc(s_state, 1)

            def state_lo(it):
                pool.wait_ge(s_hi, it.n + 1)
                pool.tensor_tensor(state16[:, 1, it.j, 1, :], state[:, 1, it.j, :],
                                   state16[:, 1, it.j, 0, :], ALU.subtract).then_inc(s_lo, 1)

            def state_normed(group, j):
                pool.wait_ge(s_state16_0, group + 1)
                pool.tensor_tensor(state[:, 0, j, :], state16[:, 0, j, 0, :], state16[:, 0, j, 1, :],
                                   ALU.add).then_inc(s_state0, 1)

            def step(st, q, prepare):
                if st.back[2] is not None:
                    state_lo(st.back[2])
                if st.back[1] is not None:
                    new_state(st.back[1])
                if prepare:
                    if st.m in STATS_AT:
                        inverse_std((q + 1) * BATCH + STATS_AT[st.m], STATS_AT[st.m])
                    if st.m in TURN0_AT:
                        state_normed((q + 1) * BATCH + TURN0_AT[st.m], TURN0_AT[st.m])
                elif isinstance(q, int) and q == 0 and st.m < LAG:
                    if st.m + 2 < BATCH:
                        inverse_std(st.m + 2, st.m + 2)
                    state_normed(st.m + 1, st.m + 1)

            setup()
            inverse_std(0, 0)
            inverse_std(1, 1)
            state_normed(0, 0)
            run(pool, step)


def kernel(**inputs):
    import numpy as np
    from concourse import bacc
    from concourse.bass_utils import run_bass_kernel_spmd

    nc = bacc.Bacc("TRN2", target_bir_lowering=False, num_devices=1)
    names = ["x", "adj", "L0_gnn_weight", "L0_gnn_w_ih", "L0_gnn_w_hh", "L0_gnn_b_ih", "L0_gnn_b_hh"]
    arrays, args = {}, []
    for name in names:
        a = np.ascontiguousarray(inputs[name])
        arrays[f"in_{name}"] = a
        args.append(nc.dram_tensor(f"in_{name}", a.shape, mybir.dt.from_np(a.dtype), kind="ExternalInput").ap())
    shape = inputs["x"].shape
    args.append(nc.dram_tensor("out_h", shape, F32, kind="ExternalOutput").ap())
    build(nc, *args)
    done = run_bass_kernel_spmd(nc, [arrays], core_ids=[0])
    return done.results[0]["out_h"]
```

```python
from contextlib import ExitStack

import concourse.bass as bass
from concourse import mybir

F32 = mybir.dt.float32
F16 = mybir.dt.float16
I32 = mybir.dt.int32
ALU = mybir.AluOpType
ACT = mybir.ActivationFunctionType
AX_X = mybir.AxisListType.X

P = 128
GPG = 4
N = GPG * P
LAYERS = 3
R, Z, NN = range(3)
GATES = 3
WHH = LAYERS
SLOTS_W = LAYERS + 1
EPS = 1e-5
H_SCALE = 2.0 ** 11
U_SCALE = 2.0 ** -6
W_TOP = 2.0 ** 13
EXPONENT_BITS = 0x7F800000

BATCH = 4
ITEMS = LAYERS * BATCH
LAG = 3
FIRST = 1
STATS_AT = {3: 0, 5: 1, 8: 2, 11: 3}
NORM_AT = {4: 0, 6: 1, 9: 2, 12: 3}
TURN0_AT = {5: 0, 7: 1, 10: 2, 13: 3}


class Item:

    def __init__(self, q, m):
        self.n = q * ITEMS + m
        self.layer = m % ITEMS // BATCH + 1
        self.j = m % BATCH
        self.group = (q + m // ITEMS) * BATCH + self.j
        self.parity = m % 2


class Step:

    def __init__(self, q, m, first=0, last=None):
        def item(i):
            return Item(q, i) if i >= first and (last is None or i <= last) else None

        self.m = m
        self.item = item(m)
        self.back = [item(m - i) for i in range(LAG + 1)]
        self.draining = last is not None and m > last
        self.first_turned = m + FIRST if last is None and isinstance(q, int) and m + FIRST < BATCH else None


def build(nc, x, adj, weight, w_ih, w_hh, b_ih, b_hh, out):
    graphs = x.shape[0]
    groups = graphs // GPG
    batches = groups // BATCH

    with ExitStack() as ctx:
        def sb(name, shape, dt):
            return ctx.enter_context(nc.sbuf_tensor(name, shape, dt))

        def psum(name):
            return ctx.enter_context(nc.psum_tensor(name, [P, N], F32))

        def sem(name):
            return ctx.enter_context(nc.semaphore(name))

        ps_r, ps_z, ps_hn = psum("ps_r"), psum("ps_z"), psum("ps_hn")
        ps_in = [psum("ps_in0"), psum("ps_in1")]
        ps_u, ps_turn, ps_turn0 = psum("ps_u"), psum("ps_turn"), psum("ps_turn0")

        x_all = sb("x_all", [P, graphs * P], F32)
        adj_int = sb("adj_int", [P, graphs * P], I32)
        adj_one = sb("adj_one", [P, graphs * P], F16)
        ident = sb("ident", [P, P], F32)
        wih_rows = sb("wih_rows", [P, GATES, P], F32)
        wl_rows = sb("wl_rows", [P, LAYERS, P], F32)
        wih_t = sb("wih_t", [P, GATES, P], F32)
        wl_t = sb("wl_t", [P, LAYERS, P], F32)
        w_rows = sb("w_rows", [P, GATES, SLOTS_W, P], F32)
        w_hi = sb("w_hi", [P, GATES, SLOTS_W, P], F16)
        w_lo = sb("w_lo", [P, GATES, SLOTS_W, P], F16)
        bias_rows = sb("bias_rows", [2 * GATES, P], F32)
        biases = sb("biases", [P, 2 * GATES], F32)
        bias_ih, bias_hh = biases[:, 0:GATES], biases[:, GATES:2 * GATES]
        w_top = sb("w_top", [P, GATES], F32)
        w_scale = sb("w_scale", [P, GATES], F32)
        back_scale = sb("back_scale", [P, GATES], F32)
        gate_bias = sb("gate_bias", [P, GATES], F32)
        neg_scale = sb("neg_scale", [P, 1], F32)
        bhn_scaled = sb("bhn_scaled", [P, 1], F32)
        half_neg = sb("half_neg", [P, GPG], F32)
        stats = sb("stats", [P, BATCH, GPG, 6], F32)
        moments = sb("moments", [P, BATCH, GPG, 2], F32)
        neg_mean = sb("neg_mean", [P, BATCH, GPG], F32)
        var_eps = sb("var_eps", [P, BATCH, GPG], F32)
        inv_std = sb("inv_std", [P, BATCH, GPG], F32)
        normed = sb("normed", [P, BATCH, N], F32)
        state = sb("state", [P, 2, BATCH, N], F32)
        state16 = sb("state16", [P, 2, BATCH, 2, N], F16)
        nodes16 = sb("nodes16", [P, 2, BATCH, 2, N], F16)
        u16 = sb("u16", [P, 2, N], F16)
        r_sb = sb("r_sb", [P, N], F32)
        z_sb = sb("z_sb", [P, 2, N], F32)
        rn_sb = sb("rn_sb", [P, N], F32)
        diff = sb("diff", [P, 2, N], F32)
        step_sb = sb("step_sb", [P, N], F32)

        s_wih, s_wl, s_whh, s_b = sem("s_wih"), sem("s_wl"), sem("s_whh"), sem("s_b")
        s_x, s_adj, s_store = sem("s_x"), sem("s_adj"), sem("s_store")
        s_x_first = [sem(f"s_x_first{j}") for j in range(BATCH)]
        s_adj_first = [sem(f"s_adj_first{j}") for j in range(BATCH)]
        s_zero, s_ident, s_half, s_scale, s_bias = (
            sem("s_zero"), sem("s_ident"), sem("s_half"), sem("s_scale"), sem("s_bias"))
        s_wt, s_wt_sb, s_prod = sem("s_wt"), sem("s_wt_sb"), sem("s_prod")
        s_rows, s_const, s_wturn, s_whi, s_wlo = (
            sem("s_rows"), sem("s_const"), sem("s_wturn"), sem("s_whi"), sem("s_wlo"))
        s_bn, s_mom, s_neg, s_var, s_inv, s_normed, s_one = (
            sem("s_bn"), sem("s_mom"), sem("s_neg"), sem("s_var"), sem("s_inv"), sem("s_normed"), sem("s_one"))
        s_nodes0_hi, s_nodes0, s_turn0, s_parts0_hi, s_parts0, s_state0 = (
            sem("s_nodes0_hi"), sem("s_nodes0"), sem("s_turn0"), sem("s_parts0_hi"), sem("s_parts0"), sem("s_state0"))
        s_agg, s_uhi, s_ulo = sem("s_agg"), sem("s_uhi"), sem("s_ulo")
        s_pr, s_pn, s_pz = sem("s_pr"), sem("s_pn"), sem("s_pz")
        s_r, s_z, s_rn, s_nsum, s_tanh = sem("s_r"), sem("s_z"), sem("s_rn"), sem("s_nsum"), sem("s_tanh")
        s_diff, s_step, s_state, s_turn = sem("s_diff"), sem("s_step"), sem("s_state"), sem("s_turn")
        s_hi, s_lo = ([sem(f"{n}{l}") for l in range(1, LAYERS)] for n in ("s_hi", "s_lo"))
        s_nodes_hi = [sem(f"s_nodes_hi{l}") for l in range(1, LAYERS)]
        s_taken = [sem(f"s_taken{l}") for l in range(1, LAYERS + 1)]

        block = ctx.enter_context(nc.Block())

        def wait_before(eng, s, value):
            if isinstance(value, int) and value <= 0:
                return
            eng.wait_ge(s, value)

        def run(eng, step):
            for m in range(LAG):
                step(Step(0, m), 0, False)
            with eng.Fori(0, batches - 1) as q:
                for m in range(LAG, ITEMS + LAG):
                    step(Step(q, m), q, True)
            for m in range(LAG, ITEMS + LAG):
                step(Step(batches - 1, m, last=ITEMS - 1), batches - 1, False)

        def group_columns(group):
            return bass.ds(group * N, N)

        @block.sync
        def _(sp):
            x_src = x.rearrange("g n d -> n g d")
            adj_src = adj.rearrange("g s t -> s g t")
            out_dst = out.rearrange("g n d -> n g d")
            sp.dma_start(wl_rows[:, :, :], weight.rearrange("l d f -> d l f")).then_inc(s_wl, 16)
            for j in range(BATCH):
                cols, src = slice(j * N, (j + 1) * N), slice(j * GPG, (j + 1) * GPG)
                sp.dma_start(x_all[:, cols].rearrange("p (g d) -> p g d", d=P), x_src[:, src, :]).then_inc(s_x_first[j], 16)
                sp.dma_start(adj_int[:, cols].rearrange("p (g d) -> p g d", d=P), adj_src[:, src, :]).then_inc(s_adj_first[j], 16)
            first_pair = BATCH // 2

            def load(pair):
                first = pair * (2 * GPG) if isinstance(pair, int) else sp.snap(pair * (2 * GPG))
                cols, src = bass.ds(first * P, 2 * N), bass.ds(first, 2 * GPG)
                if not isinstance(pair, int):
                    sp.wait_ge(s_x, (pair - first_pair) * 16)
                    sp.wait_ge(s_adj, (pair - first_pair) * 16)
                sp.dma_start(x_all[:, cols].rearrange("p (g d) -> p g d", d=P), x_src[:, src, :]).then_inc(s_x, 16)
                sp.dma_start(adj_int[:, cols].rearrange("p (g d) -> p g d", d=P), adj_src[:, src, :]).then_inc(s_adj, 16)

            load(first_pair)
            with sp.Fori(first_pair + 1, groups // 2) as pair:
                load(pair)
            with sp.Fori(0, groups) as g:
                sp.wait_ge(s_taken[LAYERS - 1], g + 1)
                sp.dma_start(out_dst[:, bass.ds(g * GPG, GPG), :],
                             x_all[:, group_columns(g)].rearrange("p (g d) -> p g d", d=P)).then_inc(s_store, 16)
            sp.wait_ge(s_store, groups * 16)

        def new_state(eng, it):
            eng.wait_ge(s_diff, it.n + 1)
            eng.wait_ge(s_z, it.n + 1)
            wait_before(eng, s_state, it.n)
            eng.tensor_tensor(step_sb[:, :], diff[:, it.parity, :], z_sb[:, it.parity, :],
                              ALU.mult).then_inc(s_step, 1)
            eng.wait_ge(s_step, it.n + 1)
            eng.tensor_tensor(state[:, 1, it.j, :], state[:, source(it), it.j, :], step_sb[:, :],
                              ALU.add).then_inc(s_state, 1)

        def source(it):
            return 0 if it.layer == 1 else 1

        def normalise(eng, group, j):
            eng.wait_ge(s_inv, group + 1)
            eng.wait_ge(s_neg, group + 1)
            for b in range(GPG):
                eng.tensor_scalar(normed[:, j, b * P:(b + 1) * P], x_all[:, bass.ds(group * N + b * P, P)],
                                  neg_mean[:, j, b:b + 1], inv_std[:, j, b:b + 1],
                                  ALU.add, ALU.mult).then_inc(s_normed, 1)

        @block.tensor
        def _(pe):
            def product(bank, gate, slot, hi, lo, first, last):
                wh, wl = w_hi[:, gate, slot, :], w_lo[:, gate, slot, :]
                pe.matmul(bank[:, :], wh, hi, start=first, stop=False)
                pe.matmul(bank[:, :], wh, lo, start=False, stop=False)
                return pe.matmul(bank[:, :], wl, hi, start=False, stop=last)

            def setup():
                pe.wait_ge(s_ident, 1)
                pe.wait_ge(s_wih, 16)
                for g in range(GATES):
                    m = pe.transpose(ps_r[:, g * P:(g + 1) * P], wih_rows[:, g, :], ident[:, :])
                m.then_inc(s_wt, 1)
                pe.wait_ge(s_wl, 16)
                for l in range(LAYERS):
                    m = pe.transpose(ps_z[:, l * P:(l + 1) * P], wl_rows[:, l, :], ident[:, :])
                m.then_inc(s_wt, 1)
                pe.wait_ge(s_wt_sb, 2)
                for g, bank in enumerate((ps_hn, ps_in[0], ps_in[1])):
                    pe.matmul(bank[:, 0:LAYERS * P], wih_t[:, g, :], wl_t[:, :, :].rearrange("p l d -> p (l d)"),
                              start=True, stop=True).then_inc(s_prod, 1)
                pe.wait_ge(s_b, 2 * 16)
                pe.transpose(ps_u[:, 0:2 * GATES], bias_rows[:, :], ident[0:2 * GATES, 0:2 * GATES]).then_inc(s_wt, 1)
                for j in range(FIRST):
                    turn_normed(j, j)
                for g, bank in enumerate((ps_r, ps_z, ps_turn)):
                    pe.wait_ge(s_rows, GATES + 1 + g)
                    for s in range(SLOTS_W):
                        m = pe.transpose(bank[:, s * P:(s + 1) * P], w_rows[:, g, s, :], ident[:, :])
                    m.then_inc(s_wturn, 1)
                pe.wait_ge(s_bias, 1)

            def aggregate(it):
                if it.layer == 1:
                    pe.wait_ge(s_nodes0, it.group + 1)
                    pe.wait_ge(s_one, it.group + 1)
                else:
                    pe.wait_ge(s_taken[it.layer - 2], it.group + 1)
                wait_before(pe, s_ulo, it.n)
                for b in range(GPG):
                    cols = slice(b * P, (b + 1) * P)
                    a = adj_one[:, bass.ds(it.group * N + b * P, P)]
                    pe.matmul(ps_u[:, cols], nodes16[:, source(it), it.j, 0, cols], a, start=True, stop=False)
                    m = pe.matmul(ps_u[:, cols], nodes16[:, source(it), it.j, 1, cols], a, start=False, stop=True)
                m.then_inc(s_agg, 1)

            def hidden_part_r(it, first_use):
                hi, lo = (state16[:, source(it), it.j, c, :] for c in (0, 1))
                if it.layer == 1:
                    pe.wait_ge(s_parts0, it.group + 1)
                else:
                    pe.wait_ge(s_lo[it.layer - 2], it.group + 1)
                wait_before(pe, s_r, it.n)
                if first_use:
                    pe.wait_ge(s_wlo, R + 1)
                product(ps_r, R, WHH, hi, lo, True, False)

            def hidden_part(it, first_use):
                hi, lo = (state16[:, source(it), it.j, c, :] for c in (0, 1))
                wait_before(pe, s_z, it.n)
                if first_use:
                    pe.wait_ge(s_wlo, Z + 1)
                product(ps_z, Z, WHH, hi, lo, True, False)
                wait_before(pe, s_rn, it.n)
                if first_use:
                    pe.wait_ge(s_wlo, NN + 1)
                product(ps_hn, NN, WHH, hi, lo, True, True)

            def input_part_r(it):
                pe.wait_ge(s_ulo, it.n + 1)
                product(ps_r, R, it.layer - 1, u16[:, 0, :], u16[:, 1, :], False, True).then_inc(s_pr, 1)

            def input_part(it):
                hi, lo, s = u16[:, 0, :], u16[:, 1, :], it.layer - 1
                product(ps_z, Z, s, hi, lo, False, True).then_inc(s_pz, 1)
                wait_before(pe, s_diff, it.n - 1)
                product(ps_in[it.parity], NN, s, hi, lo, True, True).then_inc(s_pn, 1)

            def turn(it, st):
                pe.wait_ge(s_state, it.n + 1)
                before = st.back[3]
                if before is not None:
                    pe.wait_ge(s_taken[before.layer - 1], before.group + 1)
                for b in range(GPG):
                    cols = slice(b * P, (b + 1) * P)
                    m = pe.transpose(ps_turn[:, cols], state[:, 1, it.j, cols], ident[:, :])
                m.then_inc(s_turn, 1)

            def turn_normed(group, j):
                pe.wait_ge(s_normed, (group + 1) * GPG)
                wait_before(pe, s_parts0, group)
                wait_before(pe, s_state0, group)
                for b in range(GPG):
                    cols = slice(b * P, (b + 1) * P)
                    m = pe.transpose(ps_turn0[:, cols], normed[:, j, cols], ident[:, :])
                m.then_inc(s_turn0, 1)

            def step(st, q, prepare):
                it, _, b2, _ = st.back
                if it is not None:
                    aggregate(it)
                    first_use = isinstance(it.n, int) and it.n == 0
                    hidden_part_r(it, first_use)
                    hidden_part(it, first_use)
                if prepare and st.m in TURN0_AT:
                    turn_normed((q + 1) * BATCH + TURN0_AT[st.m], TURN0_AT[st.m])
                if st.first_turned is not None:
                    turn_normed(st.first_turned, st.first_turned)
                if it is not None:
                    input_part_r(it)
                if b2 is not None:
                    turn(b2, st)
                if it is not None:
                    input_part(it)

            setup()
            run(pe, step)

        @block.scalar
        def _(act):
            def setup():
                act.dma_start(wih_rows[:, :, :], w_ih.rearrange("(g e) f -> e g f", e=P)).then_inc(s_wih, 16)
                act.wait_ge(s_half, 1)
                act.activation(r_sb[:, 0:1], half_neg[:, 0:1], ACT.Sigmoid)
                act.wait_ge(s_wt, 1)
                act.activation(wih_t[:, :, :].rearrange("p g e -> p (g e)"), ps_r[:, 0:GATES * P],
                               ACT.Copy).then_inc(s_wt_sb, 1)
                for g, bank in enumerate((ps_hn, ps_in[0], ps_in[1])):
                    act.wait_ge(s_prod, g + 1)
                    act.activation(w_rows[:, g, 0:LAYERS, :].rearrange("p l d -> p (l d)"), bank[:, 0:LAYERS * P],
                                   ACT.Copy, scale=1.0 / U_SCALE).then_inc(s_rows, 1)
                for j in range(FIRST):
                    nodes0_hi(j, j)
                    parts0_hi(j, j)
                for g, bank in enumerate((ps_r, ps_z, ps_turn)):
                    act.wait_ge(s_wturn, g + 1)
                    act.activation(w_hi[:, g, :, :].rearrange("p s e -> p (s e)"), bank[:, :],
                                   ACT.Copy).then_inc(s_whi, 1)
                for j in range(FIRST):
                    state0(j, j)

            def gate_z(it):
                act.wait_ge(s_pz, it.n + 1)
                wait_before(act, s_step, it.n - 1)
                act.activation(z_sb[:, it.parity, :], ps_z[:, :], ACT.Sigmoid,
                               bias=gate_bias[:, Z:Z + 1], scale=neg_scale[:, :]).then_inc(s_z, 1)

            def gate_r(it):
                if isinstance(it.n, int) and it.n == 0:
                    act.wait_ge(s_const, 3)
                act.wait_ge(s_pr, it.n + 1)
                wait_before(act, s_rn, it.n)
                act.activation(r_sb[:, :], ps_r[:, :], ACT.Sigmoid,
                               bias=gate_bias[:, R:R + 1], scale=back_scale[:, R:R + 1]).then_inc(s_r, 1)

            def gate_n(it):
                act.wait_ge(s_nsum, it.n + 1)
                bank = ps_in[it.parity]
                act.activation(bank[:, :], bank[:, :], ACT.Tanh,
                               bias=biases[:, NN:NN + 1], scale=back_scale[:, NN:NN + 1]).then_inc(s_tanh, 1)

            def u_hi(it):
                act.wait_ge(s_agg, it.n + 1)
                act.activation(u16[:, 0, :], ps_u[:, :], ACT.Copy, scale=U_SCALE).then_inc(s_uhi, 1)

            def state_hi(it):
                act.wait_ge(s_state, it.n + 1)
                act.activation(state16[:, 1, it.j, 0, :], state[:, 1, it.j, :], ACT.Copy).then_inc(s_hi[it.layer - 1], 1)

            def nodes_hi(it):
                act.wait_ge(s_turn, it.n + 1)
                act.activation(nodes16[:, 1, it.j, 0, :], ps_turn[:, :], ACT.Copy).then_inc(s_nodes_hi[it.layer - 1], 1)

            def nodes0_hi(group, j):
                act.wait_ge(s_normed, (group + 1) * GPG)
                act.activation(nodes16[:, 0, j, 0, :], normed[:, j, :], ACT.Relu).then_inc(s_nodes0_hi, 1)

            def parts0_hi(group, j):
                act.wait_ge(s_turn0, group + 1)
                act.activation(state16[:, 0, j, 0, :], ps_turn0[:, :], ACT.Relu).then_inc(s_parts0_hi, 1)

            def state0(group, j):
                act.wait_ge(s_parts0, group + 1)
                act.activation(state[:, 0, j, :], ps_turn0[:, :], ACT.Relu).then_inc(s_state0, 1)

            def step(st, q, prepare):
                it, b1, b2, _ = st.back
                if b1 is not None:
                    gate_z(b1)
                if it is not None:
                    u_hi(it)
                if prepare and st.m in TURN0_AT:
                    nodes0_hi((q + 1) * BATCH + TURN0_AT[st.m], TURN0_AT[st.m])
                if st.first_turned is not None:
                    nodes0_hi(st.first_turned, st.first_turned)
                if b2 is not None and b2.layer < LAYERS:
                    state_hi(b2)
                if b1 is not None:
                    gate_n(b1)
                if prepare and st.m in TURN0_AT:
                    parts0_hi((q + 1) * BATCH + TURN0_AT[st.m], TURN0_AT[st.m])
                if st.first_turned is not None:
                    parts0_hi(st.first_turned, st.first_turned)
                if prepare and st.m - 1 in TURN0_AT:
                    state0((q + 1) * BATCH + TURN0_AT[st.m - 1], TURN0_AT[st.m - 1])
                if it is not None:
                    gate_r(it)
                if b2 is not None and b2.layer < LAYERS:
                    nodes_hi(b2)
                if st.first_turned is not None:
                    state0(st.first_turned, st.first_turned)

            setup()
            run(act, step)

        @block.vector
        def _(dve):
            def setup():
                dve.memset(half_neg[:, :], -0.5).then_inc(s_half, 1)

            def turn_weights():
                dve.wait_ge(s_wt, 2)
                dve.tensor_copy(wl_t[:, :, :].rearrange("p l d -> p (l d)"), ps_z[:, 0:LAYERS * P]).then_inc(s_wt_sb, 1)

            def scale_weights():
                dve.wait_ge(s_whh, 16)
                for g in range(GATES):
                    dve.wait_ge(s_rows, g + 1)
                    dve.tensor_reduce(w_top[:, g:g + 1], w_rows[:, g, :, :].rearrange("p s d -> p (s d)"),
                                      AX_X, ALU.max, apply_absolute_value=True).then_inc(s_scale, 1)
                dve.wait_ge(s_scale, GATES)
                dve.tensor_scalar(w_top[:, :], w_top[:, :], 2.0 ** -60, 2.0 ** 60, ALU.max, ALU.min).then_inc(s_scale, 1)
                dve.wait_ge(s_scale, GATES + 1)
                top_bits = w_top[:, :].bitcast(I32)
                dve.tensor_scalar(top_bits, top_bits, EXPONENT_BITS, None, ALU.bitwise_and).then_inc(s_scale, 1)
                dve.wait_ge(s_scale, GATES + 2)
                dve.reciprocal(w_scale[:, :], w_top[:, :]).then_inc(s_scale, 1)
                dve.tensor_scalar(back_scale[:, :], w_top[:, :], 1.0 / (W_TOP * H_SCALE), None, ALU.mult).then_inc(s_scale, 1)
                dve.wait_ge(s_wt, 3)
                dve.tensor_copy(biases[:, :], ps_u[:, 0:2 * GATES]).then_inc(s_bias, 1)
                dve.wait_ge(s_scale, GATES + 4)
                for g in range(GATES):
                    rows = w_rows[:, g, :, :].rearrange("p s d -> p (s d)")
                    dve.tensor_scalar(rows, rows, w_scale[:, g:g + 1], W_TOP, ALU.mult, ALU.mult).then_inc(s_rows, 1)

            def gate_constants():
                dve.wait_ge(s_bias, 1)
                dve.tensor_tensor(gate_bias[:, :], bias_ih, bias_hh, ALU.add).then_inc(s_bias, 1)
                dve.tensor_scalar(neg_scale[:, :], back_scale[:, Z:Z + 1], -1.0, None, ALU.mult).then_inc(s_const, 1)
                dve.tensor_scalar(bhn_scaled[:, :], bias_hh[:, NN:NN + 1], w_scale[:, NN:NN + 1], W_TOP * H_SCALE,
                                  ALU.mult, ALU.mult).then_inc(s_const, 1)
                dve.wait_ge(s_bias, 2)
                dve.tensor_scalar(gate_bias[:, Z:Z + 1], gate_bias[:, Z:Z + 1], -1.0, None, ALU.mult).then_inc(s_const, 1)
                dve.wait_ge(s_const, 3)

            def split_weights(gates):
                for g in gates:
                    bank = (ps_r, ps_z, ps_turn)[g]
                    dve.wait_ge(s_whi, g + 1)
                    dve.tensor_tensor(w_lo[:, g, :, :].rearrange("p s e -> p (s e)"), bank[:, :],
                                      w_hi[:, g, :, :].rearrange("p s e -> p (s e)"), ALU.subtract).then_inc(s_wlo, 1)

            def adjacency(group):
                dve.tensor_scalar(adj_one[:, group_columns(group)], adj_int[:, group_columns(group)], 0.0, None,
                                  ALU.not_equal).then_inc(s_one, 1)

            def norm_stats(group, j):
                for b in range(GPG):
                    dve.bn_stats(stats[:, j, b, :], x_all[:, bass.ds(group * N + b * P, P)]).then_inc(s_bn, 1)

            def norm_moments(group, j):
                dve.wait_ge(s_bn, (group + 1) * GPG)
                adjacency(group)
                for b in range(GPG):
                    dve.bn_aggr(moments[:, j, b, :], stats[:, j, b, :]).then_inc(s_mom, 1)
                dve.wait_ge(s_mom, (group + 1) * GPG)
                dve.tensor_scalar(neg_mean[:, j, :], moments[:, j, :, 0], -1.0, None, ALU.mult).then_inc(s_neg, 1)
                dve.tensor_scalar(var_eps[:, j, :], moments[:, j, :, 1], EPS, H_SCALE ** -2,
                                  ALU.add, ALU.mult).then_inc(s_var, 1)

            def nodes0_lo(group, j):
                dve.wait_ge(s_nodes0_hi, group + 1)
                dve.scalar_tensor_tensor(out=nodes16[:, 0, j, 1, :], in0=normed[:, j, :], scalar=0.0,
                                         in1=nodes16[:, 0, j, 0, :], op0=ALU.max,
                                         op1=ALU.subtract).then_inc(s_nodes0, 1)

            def parts0_lo(group, j):
                dve.wait_ge(s_parts0_hi, group + 1)
                dve.scalar_tensor_tensor(out=state16[:, 0, j, 1, :], in0=ps_turn0[:, :], scalar=0.0,
                                         in1=state16[:, 0, j, 0, :], op0=ALU.max,
                                         op1=ALU.subtract).then_inc(s_parts0, 1)

            def u_lo(it):
                dve.wait_ge(s_uhi, it.n + 1)
                dve.scalar_tensor_tensor(out=u16[:, 1, :], in0=ps_u[:, :], scalar=U_SCALE, in1=u16[:, 0, :],
                                         op0=ALU.mult, op1=ALU.subtract).then_inc(s_ulo, 1)

            def reset_part(it):
                dve.wait_ge(s_r, it.n + 1)
                dve.scalar_tensor_tensor(out=rn_sb[:, :], in0=ps_hn[:, :], scalar=bhn_scaled[:, :], in1=r_sb[:, :],
                                         op0=ALU.add, op1=ALU.mult).then_inc(s_rn, 1)

            def n_sum(it):
                dve.wait_ge(s_rn, it.n + 1)
                dve.wait_ge(s_pn, it.n + 1)
                bank = ps_in[it.parity]
                dve.tensor_tensor(bank[:, :], bank[:, :], rn_sb[:, :], ALU.add).then_inc(s_nsum, 1)

            def difference(it):
                if it.layer == 1:
                    dve.wait_ge(s_state0, it.group + 1)
                wait_before(dve, s_step, it.n - 1)
                dve.wait_ge(s_tanh, it.n + 1)
                dve.scalar_tensor_tensor(out=diff[:, it.parity, :], in0=ps_in[it.parity][:, :], scalar=H_SCALE,
                                         in1=state[:, source(it), it.j, :], op0=ALU.mult,
                                         op1=ALU.subtract).then_inc(s_diff, 1)

            def nodes_lo(it):
                dve.wait_ge(s_nodes_hi[it.layer - 1], it.group + 1)
                dve.tensor_tensor(nodes16[:, 1, it.j, 1, :], ps_turn[:, :], nodes16[:, 1, it.j, 0, :],
                                  ALU.subtract).then_inc(s_taken[it.layer - 1], 1)

            def result(it):
                dve.wait_ge(s_turn, it.n + 1)
                cols = group_columns(it.group)
                dve.scalar_tensor_tensor(out=x_all[:, cols], in0=ps_turn[:, :], scalar=1.0 / H_SCALE,
                                         in1=x_all[:, cols], op0=ALU.mult, op1=ALU.add).then_inc(s_taken[LAYERS - 1], 1)

            def prepare_first(j):
                dve.wait_ge(s_x_first[j], 16)
                dve.wait_ge(s_adj_first[j], 16)
                norm_stats(j, j)
                norm_moments(j, j)

            def step(st, q, prepare):
                it, b1, _, b3 = st.back
                if b1 is not None:
                    reset_part(b1)
                    n_sum(b1)
                if it is not None:
                    u_lo(it)
                if b3 is not None:
                    if b3.layer == LAYERS:
                        result(b3)
                    else:
                        nodes_lo(b3)
                if prepare:
                    if st.m in STATS_AT:
                        loads = (q + 1) * (BATCH // 2)
                        dve.wait_ge(s_x, loads * 16)
                        dve.wait_ge(s_adj, loads * 16)
                        norm_stats((q + 1) * BATCH + STATS_AT[st.m], STATS_AT[st.m])
                    if st.m in TURN0_AT:
                        nodes0_lo((q + 1) * BATCH + TURN0_AT[st.m], TURN0_AT[st.m])
                if st.first_turned == FIRST:
                    prepare_first(2)
                if st.first_turned is not None:
                    nodes0_lo(st.first_turned, st.first_turned)
                if b1 is not None:
                    difference(b1)
                if b1 is not None and st.draining:
                    new_state(dve, b1)
                if prepare:
                    if st.m in STATS_AT:
                        norm_moments((q + 1) * BATCH + STATS_AT[st.m], STATS_AT[st.m])
                    if st.m in NORM_AT:
                        normalise(dve, (q + 1) * BATCH + NORM_AT[st.m], NORM_AT[st.m])
                    if st.m in TURN0_AT:
                        parts0_lo((q + 1) * BATCH + TURN0_AT[st.m], TURN0_AT[st.m])
                if st.first_turned is not None:
                    parts0_lo(st.first_turned, st.first_turned)
                if st.first_turned == FIRST:
                    prepare_first(BATCH - 1)

            setup()
            turn_weights()
            prepare_first(0)
            prepare_first(1)
            scale_weights()
            nodes0_lo(0, 0)
            split_weights((R,))
            parts0_lo(0, 0)
            split_weights((Z, NN))
            gate_constants()
            run(dve, step)

        @block.gpsimd
        def _(pool):
            def setup():
                pool.memset(ident[:, :], 0.0).then_inc(s_zero, 1)
                pool.wait_ge(s_zero, 1)
                pool.affine_select(out=ident[:, :], in_=ident[:, :], compare_op=ALU.not_equal, fill=1.0, base=0,
                                   pattern=[[-1, P]], channel_multiplier=1).then_inc(s_ident, 1)
                pool.dma_start(w_rows[:, :, WHH, :], w_hh.rearrange("(g e) f -> e g f", e=P)).then_inc(s_whh, 16)
                pool.dma_start(bias_rows[0:GATES, :], b_ih.rearrange("(g e) -> g e", e=P)).then_inc(s_b, 16)
                pool.dma_start(bias_rows[GATES:2 * GATES, :], b_hh.rearrange("(g e) -> g e", e=P)).then_inc(s_b, 16)
                pool.wait_ge(s_half, 1)

            def inverse_std(group, j):
                pool.wait_ge(s_var, group + 1)
                pool.tensor_tensor(inv_std[:, j, :], var_eps[:, j, :], half_neg[:, :], ALU.pow).then_inc(s_inv, 1)

            def state_lo(it):
                pool.wait_ge(s_hi[it.layer - 1], it.group + 1)
                pool.tensor_tensor(state16[:, 1, it.j, 1, :], state[:, 1, it.j, :],
                                   state16[:, 1, it.j, 0, :], ALU.subtract).then_inc(s_lo[it.layer - 1], 1)

            def step(st, q, prepare):
                _, b1, b2, _ = st.back
                if b2 is not None and b2.layer < LAYERS:
                    state_lo(b2)
                if b1 is not None and not st.draining:
                    new_state(pool, b1)
                if prepare and st.m in STATS_AT:
                    inverse_std((q + 1) * BATCH + STATS_AT[st.m], STATS_AT[st.m])

            setup()
            for j in range(BATCH):
                inverse_std(j, j)
                normalise(pool, j, j)
            run(pool, step)


def kernel(**inputs):
    import numpy as np
    from concourse import bacc
    from concourse.bass_utils import run_bass_kernel_spmd

    nc = bacc.Bacc("TRN2", target_bir_lowering=False, num_devices=1)
    names = ["x", "adj", "L0_gnn_weight", "L0_gnn_w_ih", "L0_gnn_w_hh", "L0_gnn_b_ih", "L0_gnn_b_hh"]
    arrays, args = {}, []
    for name in names:
        a = np.ascontiguousarray(inputs[name])
        arrays[f"in_{name}"] = a
        args.append(nc.dram_tensor(f"in_{name}", a.shape, mybir.dt.from_np(a.dtype), kind="ExternalInput").ap())
    shape = inputs["x"].shape
    args.append(nc.dram_tensor("out_h", shape, F32, kind="ExternalOutput").ap())
    build(nc, *args)
    done = run_bass_kernel_spmd(nc, [arrays], core_ids=[0])
    return done.results[0]["out_h"]
```
